# Optimizing a Trainium2 kernel written in Bass

```python
import numpy as np
import jax
import jax.numpy as jnp

def _softmax(x, axis=-1):
    return jax.nn.softmax(x, axis=axis)

def _gelu(x):
    return jax.nn.gelu(x, approximate=True)

def _silu(x):
    return jax.nn.silu(x)

def _sigmoid(x):
    return jax.nn.sigmoid(x)

def _layernorm(x, axis=-1, eps=1e-05):
    m = jnp.mean(x, axis=axis, keepdims=True)
    v = jnp.var(x, axis=axis, keepdims=True)
    return (x - m) / jnp.sqrt(v + eps)

def _scatter_add(tgt, idx, src, axis=0):
    return tgt.at[idx].add(src)

def _segment_sum(src, seg, n):
    return jax.ops.segment_sum(src, seg, n)
kernel_name = 'mk_pixart_seq_d4_seqx_r8_e86635'

def setup_inputs(seed: int=0):
    np.random.seed(seed)
    _w = jnp.asarray

    def _rec_inputs():
        import jax
        import jax.numpy as jnp
        _rk = jax.random.key(seed)
        x = -0.0002928 + 1 * jax.random.normal(jax.random.fold_in(_rk, 1), (4, 512, 128), jnp.float32)
        _lenS = 512 - jax.random.randint(jax.random.fold_in(_rk, 7), (4,), 0, max(1, 512 // 4) + 1, jnp.int32)
        _lenS2 = 77 - jax.random.randint(jax.random.fold_in(_rk, 8), (4,), 0, max(1, 77 // 4) + 1, jnp.int32)
        cond_1024 = 0.000887014 + 1.03683 * jax.random.normal(jax.random.fold_in(_rk, 11), (4, 128), jnp.float32)
        _ctx_1024P = jax.random.normal(jax.random.fold_in(_rk, 12), (4, 16, 128), jnp.float32)
        _ctx_1024c = jax.random.dirichlet(jax.random.fold_in(_rk, 512), 0.3 * jnp.ones((16,), jnp.float32), (4, 77))
        _ctx_1024t = jnp.einsum('bsk,bkd->bsd', _ctx_1024c, _ctx_1024P)
        _ctx_1024t = _ctx_1024t * jax.lax.rsqrt(jnp.mean(jnp.square(_ctx_1024t)) + 1e-12) * 0.953939
        ctx_1024 = -0.00606593 + 0.997213 * (_ctx_1024t + 0.3 * jax.random.normal(jax.random.fold_in(_rk, 612), (4, 77, 128), jnp.float32))
        _validS = jnp.arange(512)[None, :] < _lenS[:, None]
        _validS2 = jnp.arange(77)[None, :] < _lenS2[:, None]
        _causal = jnp.tril(jnp.ones((512, 512), dtype=bool))
        mask_BxS2_bf1 = jnp.ones((4, 77), dtype=bool)
        mask_SxS_bk0 = jnp.logical_not(jnp.broadcast_to(_validS[0:1, :], (512, 512)))
        return (x, cond_1024, ctx_1024, mask_BxS2_bf1, mask_SxS_bk0)
    x, cond_1024, ctx_1024, mask_BxS2_bf1, mask_SxS_bk0 = _rec_inputs()

    def _L0_xcond_setup():
        import jax, jax.numpy as jnp
        import numpy as np
        B, N, D, H, LC = (2, 128, 128, 16, 77)
        HD = D // H
        BLOCK = 16
        ROPE_BASE = 10000.0
        EPS = 1e-05

        def _block_diff_mask(n, block_size):
            idx = np.arange(2 * n)
            q = idx[:, None]
            kv = idx[None, :]
            fq = q >= n
            fkv = kv >= n
            bq = np.where(fq, (q - n) // block_size, q // block_size)
            bkv = np.where(fkv, (kv - n) // block_size, kv // block_size)
            block_diagonal = (bq == bkv) & (fq == fkv)
            offset_block_causal = (bq > bkv) & fkv & ~fq
            block_causal = (bq >= bkv) & fq & fkv
            return jnp.asarray(block_diagonal | offset_block_causal | block_causal)

        def _rope_tables(n):
            inv_freq = 1.0 / ROPE_BASE ** (np.arange(0, HD, 2, dtype=np.float32) / HD)
            freqs = np.outer(np.arange(n, dtype=np.float32), inv_freq)
            emb = np.concatenate([freqs, freqs], axis=-1)
            cos = jnp.asarray(np.cos(emb), jnp.float32)[None, :, None, :]
            sin = jnp.asarray(np.sin(emb), jnp.float32)[None, :, None, :]
            return (cos, sin)

        def _ln(x, w):
            xf = x.astype(jnp.float32)
            mu = jnp.mean(xf, axis=-1, keepdims=True)
            var = jnp.mean(jnp.square(xf - mu), axis=-1, keepdims=True)
            y = (xf - mu) * jax.lax.rsqrt(var + EPS)
            return y * w[None, None, :]

        def _apply_rope(t, cos, sin):
            t1, t2 = jnp.split(t, 2, axis=-1)
            rot = jnp.concatenate([-t2, t1], axis=-1)
            return t * cos + rot * sin

        def _attn(q, k, v, mask):
            scale = 1.0 / np.sqrt(HD)
            s = jnp.einsum('bqhd,bkhd->bhqk', q, k) * scale
            s = jnp.where(mask, s, jnp.finfo(s.dtype).min)
            a = jax.nn.softmax(s, axis=-1)
            return jnp.einsum('bhqk,bkhd->bqhd', a, v)
        key = jax.random.key(seed)
        ks = jax.random.split(key, 16)
        w = lambda k, shp: jax.random.normal(k, shp, jnp.float32) * 0.02
        inp = {'x': jax.random.normal(ks[0], (B, 2 * N, D), jnp.float32), 'cond_global': jax.random.normal(ks[1], (B, D), jnp.float32), 'cond_tokens': jax.random.normal(ks[2], (B, LC, D), jnp.float32), 'adaLN_W': w(ks[3], (D, 9 * D)), 'adaLN_b': w(ks[4], (9 * D,)), 'norm1_w': jnp.ones((D,), jnp.float32), 'qkv_W': w(ks[5], (D, 3 * D)), 'attn_out_W': w(ks[6], (D, D)), 'normc_w': jnp.ones((D,), jnp.float32), 'cq_W': w(ks[7], (D, D)), 'ck_W': w(ks[8], (D, D)), 'cv_W': w(ks[9], (D, D)), 'co_W': w(ks[10], (D, D)), 'norm2_w': jnp.ones((D,), jnp.float32), 'mlp_W1': w(ks[11], (D, 4 * D)), 'mlp_b1': w(ks[12], (4 * D,)), 'mlp_W2': w(ks[13], (4 * D, D)), 'mlp_b2': w(ks[14], (D,)), 'cond_kv_mask': jnp.ones((B, LC), bool), 'attn_mask': _block_diff_mask(N, BLOCK)}
        return inp
    _L0_xcond_all = _L0_xcond_setup()
    _L0_xcond_in = {k: v for k, v in _L0_xcond_all.items() if k in ('adaLN_W', 'adaLN_b', 'norm1_w', 'qkv_W', 'attn_out_W', 'normc_w', 'cq_W', 'ck_W', 'cv_W', 'co_W', 'norm2_w', 'mlp_W1', 'mlp_b1', 'mlp_W2', 'mlp_b2')}
    del _L0_xcond_all

    def _L1_xcond_setup():
        import jax, jax.numpy as jnp
        import numpy as np
        C = 128
        H = 16
        D = C // H
        WIN = 64
        SHIFT = 32
        TOPK = 16
        HID = 512
        EPS = 1e-06

        def _ln(x):
            x32 = x.astype(jnp.float32)
            m = x32.mean(-1, keepdims=True)
            v = jnp.mean((x32 - m) ** 2, axis=-1, keepdims=True)
            return ((x32 - m) * jax.lax.rsqrt(v + EPS)).astype(x.dtype)

        def _self_attn(h, w_qkv, b_qkv, w_so, b_so):
            B, L, _ = h.shape
            qkv = h @ w_qkv + b_qkv
            qkv = jnp.roll(qkv, -SHIFT, axis=1)
            nw = L // WIN
            qkv = qkv.reshape(B, nw, WIN, 3, H, D)
            q, k, v = (qkv[:, :, :, 0], qkv[:, :, :, 1], qkv[:, :, :, 2])
            scores = jnp.einsum('bnqhd,bnkhd->bnhqk', q, k) / jnp.sqrt(jnp.float32(D)).astype(h.dtype)
            attn = jax.nn.softmax(scores, axis=-1)
            o = jnp.einsum('bnhqk,bnkhd->bnqhd', attn, v).reshape(B, L, C)
            o = jnp.roll(o, SHIFT, axis=1)
            return o @ w_so + b_so

        def _topk_cross_attn(h, ctx, w_q, b_q, w_kv, b_kv, w_co, b_co):
            B, L, _ = h.shape
            Lc = ctx.shape[1]
            q = (h @ w_q + b_q).reshape(B, L, H, D)
            kv = (ctx @ w_kv + b_kv).reshape(B, Lc, 2, H, D)
            k, v = (kv[:, :, 0], kv[:, :, 1])
            scores = jnp.einsum('bqhd,bkhd->bhqk', q, k) / jnp.sqrt(jnp.float32(D)).astype(h.dtype)
            top_s, top_i = jax.lax.top_k(scores, TOPK)
            attn = jax.nn.softmax(top_s, axis=-1)
            v_bh = jnp.transpose(v, (0, 2, 1, 3))
            vg = jnp.take_along_axis(v_bh[:, :, None, :, :], top_i[..., None], axis=3)
            o = jnp.einsum('bhqk,bhqkd->bqhd', attn, vg).reshape(B, L, C)
            return o @ w_co + b_co

        def _swiglu(h, w_m1, b_m1, w_m2, b_m2):
            u = h @ w_m1 + b_m1
            a, b = (u[..., :HID], u[..., HID:])
            return jax.nn.silu(a) * b @ w_m2 + b_m2
        key = jax.random.key(seed)
        ks = jax.random.split(key, 24)
        s = 0.02
        inp = {'x': jax.random.normal(ks[0], (2, 512, C), jnp.float32), 'mod': jax.random.normal(ks[1], (2, C), jnp.float32), 'context': jax.random.normal(ks[2], (2, 128, C), jnp.float32), 'w_ada': jax.random.normal(ks[3], (C, 9 * C), jnp.float32) * s, 'b_ada': jnp.zeros((9 * C,), jnp.float32), 'w_qkv': jax.random.normal(ks[4], (C, 3 * C), jnp.float32) * s, 'b_qkv': jnp.zeros((3 * C,), jnp.float32), 'w_so': jax.random.normal(ks[5], (C, C), jnp.float32) * s, 'b_so': jnp.zeros((C,), jnp.float32), 'w_q': jax.random.normal(ks[6], (C, C), jnp.float32) * s, 'b_q': jnp.zeros((C,), jnp.float32), 'w_kv': jax.random.normal(ks[7], (C, 2 * C), jnp.float32) * s, 'b_kv': jnp.zeros((2 * C,), jnp.float32), 'w_co': jax.random.normal(ks[8], (C, C), jnp.float32) * s, 'b_co': jnp.zeros((C,), jnp.float32), 'w_m1': jax.random.normal(ks[9], (C, 2 * HID), jnp.float32) * s, 'b_m1': jnp.zeros((2 * HID,), jnp.float32), 'w_m2': jax.random.normal(ks[10], (HID, C), jnp.float32) * s, 'b_m2': jnp.zeros((C,), jnp.float32)}
        return inp
    _L1_xcond_all = _L1_xcond_setup()
    _L1_xcond_in = {k: v for k, v in _L1_xcond_all.items() if k in ('w_ada', 'b_ada', 'w_qkv', 'b_qkv', 'w_so', 'b_so', 'w_q', 'b_q', 'w_kv', 'b_kv', 'w_co', 'b_co', 'w_m1', 'b_m1', 'w_m2', 'b_m2')}
    del _L1_xcond_all

    def _L2_xcond_setup():
        import jax, jax.numpy as jnp
        import numpy as np
        EPS = 1e-05

        def _ada_ln(x, c, W_ss, b_ss):
            mu = jnp.mean(x, axis=-1, keepdims=True)
            var = jnp.mean((x - mu) ** 2, axis=-1, keepdims=True)
            h = (x - mu) / jnp.sqrt(var + EPS)
            ss = jax.nn.silu(c) @ W_ss + b_ss
            scale, bias = jnp.split(ss, 2, axis=-1)
            return (1.0 + scale)[:, None, :] * h + bias[:, None, :]
        key = jax.random.key(seed)
        ks = jax.random.split(key, 12)
        B, Lq, Lkv, H = (8, 256, 64, 128)
        s = 0.02
        return {'x_q': jax.random.normal(ks[0], (B, Lq, H), jnp.float32), 'x_kv': jax.random.normal(ks[1], (B, Lkv, H), jnp.float32), 't_vec': jax.random.normal(ks[2], (B, H), jnp.float32), 'Wq': jax.random.normal(ks[3], (H, H), jnp.float32) * s, 'bq': jnp.zeros((H,), jnp.float32), 'Wkv': jax.random.normal(ks[4], (H, 2 * H), jnp.float32) * s, 'bkv': jnp.zeros((2 * H,), jnp.float32), 'Wp': jax.random.normal(ks[5], (H, H), jnp.float32) * s, 'bp': jnp.zeros((H,), jnp.float32), 'Wss_q': jax.random.normal(ks[6], (H, 2 * H), jnp.float32) * s, 'bss_q': jnp.zeros((2 * H,), jnp.float32), 'Wss_kv': jax.random.normal(ks[7], (H, 2 * H), jnp.float32) * s, 'bss_kv': jnp.zeros((2 * H,), jnp.float32)}
    _L2_xcond_all = _L2_xcond_setup()
    _L2_xcond_in = {k: v for k, v in _L2_xcond_all.items() if k in ('Wq', 'bq', 'Wkv', 'bkv', 'Wp', 'bp', 'Wss_q', 'bss_q', 'Wss_kv', 'bss_kv')}
    del _L2_xcond_all

    def _L3_xcond_setup():
        import jax, jax.numpy as jnp
        import numpy as np
        EPS = 1e-06
        H = 16

        def layer_norm(x, gamma=None, beta=None):
            x32 = x.astype(jnp.float32)
            mu = jnp.mean(x32, axis=-1, keepdims=True)
            var = jnp.var(x32, axis=-1, keepdims=True)
            y = (x32 - mu) * jax.lax.rsqrt(var + EPS)
            if gamma is not None:
                y = y * gamma + beta
            return y.astype(x.dtype)

        def mha(q, k, v):
            B, Nq, C = q.shape
            d = C // H
            qh = q.reshape(B, Nq, H, d)
            kh = k.reshape(B, k.shape[1], H, d)
            vh = v.reshape(B, v.shape[1], H, d)
            scores = jnp.einsum('bqhd,bkhd->bhqk', qh, kh) / jnp.sqrt(jnp.asarray(d, q.dtype))
            attn = jax.nn.softmax(scores, axis=-1)
            out = jnp.einsum('bhqk,bkhd->bqhd', attn, vh)
            return out.reshape(B, Nq, C)
        key = jax.random.key(seed)
        ks = jax.random.split(key, 24)
        B, N, C, M, Cc = (4, 256, 128, 128, 128)
        hid = 4 * C
        s = 0.02
        return {'x': jax.random.normal(ks[0], (B, N, C), jnp.float32), 'mod': jax.random.normal(ks[1], (B, C), jnp.float32), 'context': jax.random.normal(ks[2], (B, M, Cc), jnp.float32), 'ada_w': jax.random.normal(ks[3], (C, 6 * C), jnp.float32) * s, 'ada_b': jnp.zeros((6 * C,), jnp.float32), 'qkv_w': jax.random.normal(ks[4], (C, 3 * C), jnp.float32) * s, 'qkv_b': jnp.zeros((3 * C,), jnp.float32), 'self_o_w': jax.random.normal(ks[5], (C, C), jnp.float32) * s, 'self_o_b': jnp.zeros((C,), jnp.float32), 'norm2_g': jnp.ones((C,), jnp.float32), 'norm2_b': jnp.zeros((C,), jnp.float32), 'q_w': jax.random.normal(ks[6], (C, C), jnp.float32) * s, 'q_b': jnp.zeros((C,), jnp.float32), 'kv_w': jax.random.normal(ks[7], (Cc, 2 * C), jnp.float32) * s, 'kv_b': jnp.zeros((2 * C,), jnp.float32), 'cross_o_w': jax.random.normal(ks[8], (C, C), jnp.float32) * s, 'cross_o_b': jnp.zeros((C,), jnp.float32), 'mlp_w1': jax.random.normal(ks[9], (C, hid), jnp.float32) * s, 'mlp_b1': jnp.zeros((hid,), jnp.float32), 'mlp_w2': jax.random.normal(ks[10], (hid, C), jnp.float32) * s, 'mlp_b2': jnp.zeros((C,), jnp.float32)}
    _L3_xcond_all = _L3_xcond_setup()
    _L3_xcond_in = {k: v for k, v in _L3_xcond_all.items() if k in ('ada_w', 'ada_b', 'qkv_w', 'qkv_b', 'self_o_w', 'self_o_b', 'norm2_g', 'norm2_b', 'q_w', 'q_b', 'kv_w', 'kv_b', 'cross_o_w', 'cross_o_b', 'mlp_w1', 'mlp_b1', 'mlp_w2', 'mlp_b2')}
    del _L3_xcond_all
    return {'x': x, 'cond_1024': cond_1024, 'ctx_1024': ctx_1024, 'mask_BxS2_bf1': mask_BxS2_bf1, 'mask_SxS_bk0': mask_SxS_bk0, 'L0_xcond_adaLN_W': _L0_xcond_in['adaLN_W'], 'L0_xcond_adaLN_b': _L0_xcond_in['adaLN_b'], 'L0_xcond_norm1_w': _L0_xcond_in['norm1_w'], 'L0_xcond_qkv_W': _L0_xcond_in['qkv_W'], 'L0_xcond_attn_out_W': _L0_xcond_in['attn_out_W'], 'L0_xcond_normc_w': _L0_xcond_in['normc_w'], 'L0_xcond_cq_W': _L0_xcond_in['cq_W'], 'L0_xcond_ck_W': _L0_xcond_in['ck_W'], 'L0_xcond_cv_W': _L0_xcond_in['cv_W'], 'L0_xcond_co_W': _L0_xcond_in['co_W'], 'L0_xcond_norm2_w': _L0_xcond_in['norm2_w'], 'L0_xcond_mlp_W1': _L0_xcond_in['mlp_W1'], 'L0_xcond_mlp_b1': _L0_xcond_in['mlp_b1'], 'L0_xcond_mlp_W2': _L0_xcond_in['mlp_W2'], 'L0_xcond_mlp_b2': _L0_xcond_in['mlp_b2'], 'L1_xcond_w_ada': _L1_xcond_in['w_ada'], 'L1_xcond_b_ada': _L1_xcond_in['b_ada'], 'L1_xcond_w_qkv': _L1_xcond_in['w_qkv'], 'L1_xcond_b_qkv': _L1_xcond_in['b_qkv'], 'L1_xcond_w_so': _L1_xcond_in['w_so'], 'L1_xcond_b_so': _L1_xcond_in['b_so'], 'L1_xcond_w_q': _L1_xcond_in['w_q'], 'L1_xcond_b_q': _L1_xcond_in['b_q'], 'L1_xcond_w_kv': _L1_xcond_in['w_kv'], 'L1_xcond_b_kv': _L1_xcond_in['b_kv'], 'L1_xcond_w_co': _L1_xcond_in['w_co'], 'L1_xcond_b_co': _L1_xcond_in['b_co'], 'L1_xcond_w_m1': _L1_xcond_in['w_m1'], 'L1_xcond_b_m1': _L1_xcond_in['b_m1'], 'L1_xcond_w_m2': _L1_xcond_in['w_m2'], 'L1_xcond_b_m2': _L1_xcond_in['b_m2'], 'L2_xcond_Wq': _L2_xcond_in['Wq'], 'L2_xcond_bq': _L2_xcond_in['bq'], 'L2_xcond_Wkv': _L2_xcond_in['Wkv'], 'L2_xcond_bkv': _L2_xcond_in['bkv'], 'L2_xcond_Wp': _L2_xcond_in['Wp'], 'L2_xcond_bp': _L2_xcond_in['bp'], 'L2_xcond_Wss_q': _L2_xcond_in['Wss_q'], 'L2_xcond_bss_q': _L2_xcond_in['bss_q'], 'L2_xcond_Wss_kv': _L2_xcond_in['Wss_kv'], 'L2_xcond_bss_kv': _L2_xcond_in['bss_kv'], 'L3_xcond_ada_w': _L3_xcond_in['ada_w'], 'L3_xcond_ada_b': _L3_xcond_in['ada_b'], 'L3_xcond_qkv_w': _L3_xcond_in['qkv_w'], 'L3_xcond_qkv_b': _L3_xcond_in['qkv_b'], 'L3_xcond_self_o_w': _L3_xcond_in['self_o_w'], 'L3_xcond_self_o_b': _L3_xcond_in['self_o_b'], 'L3_xcond_norm2_g': _L3_xcond_in['norm2_g'], 'L3_xcond_norm2_b': _L3_xcond_in['norm2_b'], 'L3_xcond_q_w': _L3_xcond_in['q_w'], 'L3_xcond_q_b': _L3_xcond_in['q_b'], 'L3_xcond_kv_w': _L3_xcond_in['kv_w'], 'L3_xcond_kv_b': _L3_xcond_in['kv_b'], 'L3_xcond_cross_o_w': _L3_xcond_in['cross_o_w'], 'L3_xcond_cross_o_b': _L3_xcond_in['cross_o_b'], 'L3_xcond_mlp_w1': _L3_xcond_in['mlp_w1'], 'L3_xcond_mlp_b1': _L3_xcond_in['mlp_b1'], 'L3_xcond_mlp_w2': _L3_xcond_in['mlp_w2'], 'L3_xcond_mlp_b2': _L3_xcond_in['mlp_b2']}

def reference(x, cond_1024, ctx_1024, mask_BxS2_bf1, mask_SxS_bk0, L0_xcond_adaLN_W, L0_xcond_adaLN_b, L0_xcond_norm1_w, L0_xcond_qkv_W, L0_xcond_attn_out_W, L0_xcond_normc_w, L0_xcond_cq_W, L0_xcond_ck_W, L0_xcond_cv_W, L0_xcond_co_W, L0_xcond_norm2_w, L0_xcond_mlp_W1, L0_xcond_mlp_b1, L0_xcond_mlp_W2, L0_xcond_mlp_b2, L1_xcond_w_ada, L1_xcond_b_ada, L1_xcond_w_qkv, L1_xcond_b_qkv, L1_xcond_w_so, L1_xcond_b_so, L1_xcond_w_q, L1_xcond_b_q, L1_xcond_w_kv, L1_xcond_b_kv, L1_xcond_w_co, L1_xcond_b_co, L1_xcond_w_m1, L1_xcond_b_m1, L1_xcond_w_m2, L1_xcond_b_m2, L2_xcond_Wq, L2_xcond_bq, L2_xcond_Wkv, L2_xcond_bkv, L2_xcond_Wp, L2_xcond_bp, L2_xcond_Wss_q, L2_xcond_bss_q, L2_xcond_Wss_kv, L2_xcond_bss_kv, L3_xcond_ada_w, L3_xcond_ada_b, L3_xcond_qkv_w, L3_xcond_qkv_b, L3_xcond_self_o_w, L3_xcond_self_o_b, L3_xcond_norm2_g, L3_xcond_norm2_b, L3_xcond_q_w, L3_xcond_q_b, L3_xcond_kv_w, L3_xcond_kv_b, L3_xcond_cross_o_w, L3_xcond_cross_o_b, L3_xcond_mlp_w1, L3_xcond_mlp_b1, L3_xcond_mlp_w2, L3_xcond_mlp_b2):
    import jax
    import jax.numpy as jnp

    def _L0_xcond_ref(x, cond_global, cond_tokens, adaLN_W, adaLN_b, norm1_w, qkv_W, attn_out_W, normc_w, cq_W, ck_W, cv_W, co_W, norm2_w, mlp_W1, mlp_b1, mlp_W2, mlp_b2, cond_kv_mask, attn_mask):
        import jax, jax.numpy as jnp
        import numpy as np
        B, N, D, H, LC = (2, 128, 128, 16, 77)
        HD = D // H
        BLOCK = 16
        ROPE_BASE = 10000.0
        EPS = 1e-05

        def _block_diff_mask(n, block_size):
            idx = np.arange(2 * n)
            q = idx[:, None]
            kv = idx[None, :]
            fq = q >= n
            fkv = kv >= n
            bq = np.where(fq, (q - n) // block_size, q // block_size)
            bkv = np.where(fkv, (kv - n) // block_size, kv // block_size)
            block_diagonal = (bq == bkv) & (fq == fkv)
            offset_block_causal = (bq > bkv) & fkv & ~fq
            block_causal = (bq >= bkv) & fq & fkv
            return jnp.asarray(block_diagonal | offset_block_causal | block_causal)

        def _rope_tables(n):
            inv_freq = 1.0 / ROPE_BASE ** (np.arange(0, HD, 2, dtype=np.float32) / HD)
            freqs = np.outer(np.arange(n, dtype=np.float32), inv_freq)
            emb = np.concatenate([freqs, freqs], axis=-1)
            cos = jnp.asarray(np.cos(emb), jnp.float32)[None, :, None, :]
            sin = jnp.asarray(np.sin(emb), jnp.float32)[None, :, None, :]
            return (cos, sin)

        def _ln(x, w):
            xf = x.astype(jnp.float32)
            mu = jnp.mean(xf, axis=-1, keepdims=True)
            var = jnp.mean(jnp.square(xf - mu), axis=-1, keepdims=True)
            y = (xf - mu) * jax.lax.rsqrt(var + EPS)
            return y * w[None, None, :]

        def _apply_rope(t, cos, sin):
            t1, t2 = jnp.split(t, 2, axis=-1)
            rot = jnp.concatenate([-t2, t1], axis=-1)
            return t * cos + rot * sin

        def _attn(q, k, v, mask):
            scale = 1.0 / np.sqrt(HD)
            s = jnp.einsum('bqhd,bkhd->bhqk', q, k) * scale
            s = jnp.where(mask, s, jnp.finfo(s.dtype).min)
            a = jax.nn.softmax(s, axis=-1)
            return jnp.einsum('bhqk,bkhd->bqhd', a, v)
        b, s, d = x.shape
        n = s // 2
        mod = (cond_global @ adaLN_W + adaLN_b)[:, None, :]
        sh_msa, sc_msa, g_msa, sh_x, sc_x, g_x, sh_mlp, sc_mlp, g_mlp = jnp.split(mod, 9, axis=-1)
        x_norm = _ln(x, norm1_w) * (1 + sc_msa) + sh_msa
        cos, sin = _rope_tables(n)

        def qkv(h):
            t = (h @ qkv_W).reshape(b, n, 3, H, HD)
            q, k, v = (t[:, :, 0], t[:, :, 1], t[:, :, 2])
            return (_apply_rope(q, cos, sin), _apply_rope(k, cos, sin), v)
        q1, k1, v1 = qkv(x_norm[:, :n])
        q2, k2, v2 = qkv(x_norm[:, n:])
        q = jnp.concatenate([q1, q2], axis=1)
        k = jnp.concatenate([k1, k2], axis=1)
        v = jnp.concatenate([v1, v2], axis=1)
        self_out = _attn(q, k, v, attn_mask[None, None]).reshape(b, s, d) @ attn_out_W
        x = x + g_msa * self_out
        xc = _ln(x, normc_w) * (1 + sc_x) + sh_x
        qc = (xc @ cq_W).reshape(b, s, H, HD)
        kc = (cond_tokens @ ck_W).reshape(b, LC, H, HD)
        vc = (cond_tokens @ cv_W).reshape(b, LC, H, HD)
        cross = _attn(qc, kc, vc, cond_kv_mask[:, None, None, :]).reshape(b, s, d) @ co_W
        x = x + g_x * cross
        xm = _ln(x, norm2_w) * (1 + sc_mlp) + sh_mlp
        h = jax.nn.gelu(xm @ mlp_W1 + mlp_b1, approximate=True)
        mlp_out = h @ mlp_W2 + mlp_b2
        return x + g_mlp * mlp_out

    def _L1_xcond_ref(x, mod, context, w_ada, b_ada, w_qkv, b_qkv, w_so, b_so, w_q, b_q, w_kv, b_kv, w_co, b_co, w_m1, b_m1, w_m2, b_m2):
        import jax, jax.numpy as jnp
        import numpy as np
        C = 128
        H = 16
        D = C // H
        WIN = 64
        SHIFT = 32
        TOPK = 16
        HID = 512
        EPS = 1e-06

        def _ln(x):
            x32 = x.astype(jnp.float32)
            m = x32.mean(-1, keepdims=True)
            v = jnp.mean((x32 - m) ** 2, axis=-1, keepdims=True)
            return ((x32 - m) * jax.lax.rsqrt(v + EPS)).astype(x.dtype)

        def _self_attn(h, w_qkv, b_qkv, w_so, b_so):
            B, L, _ = h.shape
            qkv = h @ w_qkv + b_qkv
            qkv = jnp.roll(qkv, -SHIFT, axis=1)
            nw = L // WIN
            qkv = qkv.reshape(B, nw, WIN, 3, H, D)
            q, k, v = (qkv[:, :, :, 0], qkv[:, :, :, 1], qkv[:, :, :, 2])
            scores = jnp.einsum('bnqhd,bnkhd->bnhqk', q, k) / jnp.sqrt(jnp.float32(D)).astype(h.dtype)
            attn = jax.nn.softmax(scores, axis=-1)
            o = jnp.einsum('bnhqk,bnkhd->bnqhd', attn, v).reshape(B, L, C)
            o = jnp.roll(o, SHIFT, axis=1)
            return o @ w_so + b_so

        def _topk_cross_attn(h, ctx, w_q, b_q, w_kv, b_kv, w_co, b_co):
            B, L, _ = h.shape
            Lc = ctx.shape[1]
            q = (h @ w_q + b_q).reshape(B, L, H, D)
            kv = (ctx @ w_kv + b_kv).reshape(B, Lc, 2, H, D)
            k, v = (kv[:, :, 0], kv[:, :, 1])
            scores = jnp.einsum('bqhd,bkhd->bhqk', q, k) / jnp.sqrt(jnp.float32(D)).astype(h.dtype)
            top_s, top_i = jax.lax.top_k(scores, TOPK)
            attn = jax.nn.softmax(top_s, axis=-1)
            v_bh = jnp.transpose(v, (0, 2, 1, 3))
            vg = jnp.take_along_axis(v_bh[:, :, None, :, :], top_i[..., None], axis=3)
            o = jnp.einsum('bhqk,bhqkd->bqhd', attn, vg).reshape(B, L, C)
            return o @ w_co + b_co

        def _swiglu(h, w_m1, b_m1, w_m2, b_m2):
            u = h @ w_m1 + b_m1
            a, b = (u[..., :HID], u[..., HID:])
            return jax.nn.silu(a) * b @ w_m2 + b_m2
        m = jax.nn.silu(mod) @ w_ada + b_ada
        sh_msa, sc_msa, g_msa, sh_mca, sc_mca, g_mca, sh_mlp, sc_mlp, g_mlp = [m[:, i * C:(i + 1) * C][:, None, :] for i in range(9)]
        h = _ln(x) * (1 + sc_msa) + sh_msa
        h = _self_attn(h, w_qkv, b_qkv, w_so, b_so)
        x = x + h * g_msa
        h = _ln(x) * (1 + sc_mca) + sh_mca
        h = _topk_cross_attn(h, context, w_q, b_q, w_kv, b_kv, w_co, b_co)
        x = x + h * g_mca
        h = _ln(x) * (1 + sc_mlp) + sh_mlp
        h = _swiglu(h, w_m1, b_m1, w_m2, b_m2)
        x = x + h * g_mlp
        return x

    def _L2_xcond_ref(x_q, x_kv, t_vec, Wq, bq, Wkv, bkv, Wp, bp, Wss_q, bss_q, Wss_kv, bss_kv):
        import jax, jax.numpy as jnp
        import numpy as np
        EPS = 1e-05

        def _ada_ln(x, c, W_ss, b_ss):
            mu = jnp.mean(x, axis=-1, keepdims=True)
            var = jnp.mean((x - mu) ** 2, axis=-1, keepdims=True)
            h = (x - mu) / jnp.sqrt(var + EPS)
            ss = jax.nn.silu(c) @ W_ss + b_ss
            scale, bias = jnp.split(ss, 2, axis=-1)
            return (1.0 + scale)[:, None, :] * h + bias[:, None, :]
        B, Lq, H = x_q.shape
        Lkv = x_kv.shape[1]
        nh = 16
        dh = H // nh
        xq = _ada_ln(x_q, t_vec, Wss_q, bss_q)
        xkv = _ada_ln(x_kv, t_vec, Wss_kv, bss_kv)
        q = (xq @ Wq + bq).reshape(B, Lq, nh, dh)
        kv = (xkv @ Wkv + bkv).reshape(B, Lkv, 2, nh, dh)
        k = kv[:, :, 0]
        v = kv[:, :, 1]
        scores = jnp.einsum('bqhd,bkhd->bhqk', q, k) / jnp.sqrt(jnp.float32(dh))
        attn = jax.nn.softmax(scores, axis=-1)
        out = jnp.einsum('bhqk,bkhd->bqhd', attn, v).reshape(B, Lq, H)
        return x_q + (out @ Wp + bp)

    def _L3_xcond_ref(x, mod, context, ada_w, ada_b, qkv_w, qkv_b, self_o_w, self_o_b, norm2_g, norm2_b, q_w, q_b, kv_w, kv_b, cross_o_w, cross_o_b, mlp_w1, mlp_b1, mlp_w2, mlp_b2):
        import jax, jax.numpy as jnp
        import numpy as np
        EPS = 1e-06
        H = 16

        def layer_norm(x, gamma=None, beta=None):
            x32 = x.astype(jnp.float32)
            mu = jnp.mean(x32, axis=-1, keepdims=True)
            var = jnp.var(x32, axis=-1, keepdims=True)
            y = (x32 - mu) * jax.lax.rsqrt(var + EPS)
            if gamma is not None:
                y = y * gamma + beta
            return y.astype(x.dtype)

        def mha(q, k, v):
            B, Nq, C = q.shape
            d = C // H
            qh = q.reshape(B, Nq, H, d)
            kh = k.reshape(B, k.shape[1], H, d)
            vh = v.reshape(B, v.shape[1], H, d)
            scores = jnp.einsum('bqhd,bkhd->bhqk', qh, kh) / jnp.sqrt(jnp.asarray(d, q.dtype))
            attn = jax.nn.softmax(scores, axis=-1)
            out = jnp.einsum('bhqk,bkhd->bqhd', attn, vh)
            return out.reshape(B, Nq, C)
        C = x.shape[-1]
        m = jax.nn.silu(mod) @ ada_w + ada_b
        shift_msa, scale_msa, gate_msa, shift_mlp, scale_mlp, gate_mlp = [c[:, None, :] for c in jnp.split(m, 6, axis=-1)]
        h = layer_norm(x)
        h = h * (1.0 + scale_msa) + shift_msa
        qkv = h @ qkv_w + qkv_b
        q, k, v = jnp.split(qkv, 3, axis=-1)
        h = mha(q, k, v) @ self_o_w + self_o_b
        x = x + h * gate_msa
        h = layer_norm(x, norm2_g, norm2_b)
        q = h @ q_w + q_b
        kv = context @ kv_w + kv_b
        k, v = jnp.split(kv, 2, axis=-1)
        h = mha(q, k, v) @ cross_o_w + cross_o_b
        x = x + h
        h = layer_norm(x)
        h = h * (1.0 + scale_mlp) + shift_mlp
        h = jax.nn.gelu(h @ mlp_w1 + mlp_b1) @ mlp_w2 + mlp_b2
        x = x + h * gate_mlp
        return x
    x = _L0_xcond_ref(x, cond_1024, ctx_1024, L0_xcond_adaLN_W, L0_xcond_adaLN_b, L0_xcond_norm1_w, L0_xcond_qkv_W, L0_xcond_attn_out_W, L0_xcond_normc_w, L0_xcond_cq_W, L0_xcond_ck_W, L0_xcond_cv_W, L0_xcond_co_W, L0_xcond_norm2_w, L0_xcond_mlp_W1, L0_xcond_mlp_b1, L0_xcond_mlp_W2, L0_xcond_mlp_b2, mask_BxS2_bf1, mask_SxS_bk0)
    x = _L1_xcond_ref(x, cond_1024, ctx_1024, L1_xcond_w_ada, L1_xcond_b_ada, L1_xcond_w_qkv, L1_xcond_b_qkv, L1_xcond_w_so, L1_xcond_b_so, L1_xcond_w_q, L1_xcond_b_q, L1_xcond_w_kv, L1_xcond_b_kv, L1_xcond_w_co, L1_xcond_b_co, L1_xcond_w_m1, L1_xcond_b_m1, L1_xcond_w_m2, L1_xcond_b_m2)
    x = _L2_xcond_ref(x, ctx_1024, cond_1024, L2_xcond_Wq, L2_xcond_bq, L2_xcond_Wkv, L2_xcond_bkv, L2_xcond_Wp, L2_xcond_bp, L2_xcond_Wss_q, L2_xcond_bss_q, L2_xcond_Wss_kv, L2_xcond_bss_kv)
    x = _L3_xcond_ref(x, cond_1024, ctx_1024, L3_xcond_ada_w, L3_xcond_ada_b, L3_xcond_qkv_w, L3_xcond_qkv_b, L3_xcond_self_o_w, L3_xcond_self_o_b, L3_xcond_norm2_g, L3_xcond_norm2_b, L3_xcond_q_w, L3_xcond_q_b, L3_xcond_kv_w, L3_xcond_kv_b, L3_xcond_cross_o_w, L3_xcond_cross_o_b, L3_xcond_mlp_w1, L3_xcond_mlp_b1, L3_xcond_mlp_w2, L3_xcond_mlp_b2)
    return x

_drawn_inputs = setup_inputs


def setup_inputs(seed=0):
    import zlib

    import numpy as np

    out = dict(_drawn_inputs(seed))
    spreads = {'L0_xcond_norm1_w': (1.0, 0.6),
     'L0_xcond_normc_w': (1.0, 0.6),
     'L0_xcond_norm2_w': (1.0, 0.6),
     'L1_xcond_b_ada': (0.0, 0.569),
     'L1_xcond_b_qkv': (0.0, 0.8),
     'L1_xcond_b_so': (0.0, 0.521),
     'L1_xcond_b_q': (0.0, 0.8),
     'L1_xcond_b_kv': (0.0, 0.8),
     'L1_xcond_b_co': (0.0, 0.48),
     'L1_xcond_b_m1': (0.0, 0.8),
     'L1_xcond_b_m2': (0.0, 1.774),
     'L2_xcond_bq': (0.0, 2.0),
     'L2_xcond_bkv': (0.0, 2.0),
     'L2_xcond_bp': (0.0, 0.8),
     'L2_xcond_bss_q': (0.0, 2.0),
     'L2_xcond_bss_kv': (0.0, 2.0),
     'L3_xcond_ada_b': (0.0, 0.523),
     'L3_xcond_qkv_b': (0.0, 0.8),
     'L3_xcond_self_o_b': (0.0, 1.499),
     'L3_xcond_norm2_g': (1.0, 0.6),
     'L3_xcond_norm2_b': (0.0, 2.0),
     'L3_xcond_q_b': (0.0, 2.0),
     'L3_xcond_kv_b': (0.0, 2.0),
     'L3_xcond_cross_o_b': (0.0, 0.8),
     'L3_xcond_mlp_b1': (0.0, 2.0),
     'L3_xcond_mlp_b2': (0.0, 1.83)}
    factors = {'L0_xcond_adaLN_W': 3.519,
     'L0_xcond_adaLN_b': 8.0,
     'L0_xcond_qkv_W': 8.0,
     'L0_xcond_attn_out_W': 8.0,
     'L0_xcond_cq_W': 8.0,
     'L0_xcond_ck_W': 8.0,
     'L0_xcond_cv_W': 8.0,
     'L0_xcond_co_W': 8.0,
     'L0_xcond_mlp_W1': 4.349,
     'L0_xcond_mlp_b1': 8.0,
     'L0_xcond_mlp_W2': 4.246,
     'L0_xcond_mlp_b2': 8.0,
     'L1_xcond_w_qkv': 8.0,
     'L1_xcond_w_so': 8.0,
     'L1_xcond_w_q': 8.0,
     'L1_xcond_w_kv': 8.0,
     'L1_xcond_w_co': 8.0,
     'L1_xcond_w_m1': 8.0,
     'L1_xcond_w_m2': 8.0,
     'L2_xcond_Wq': 64.0,
     'L2_xcond_Wss_q': 64.0,
     'L2_xcond_Wss_kv': 57.296,
     'L3_xcond_qkv_w': 8.0,
     'L3_xcond_self_o_w': 8.0,
     'L3_xcond_q_w': 64.0,
     'L3_xcond_mlp_w1': 5.921,
     'L3_xcond_mlp_w2': 5.468,
     'L2_xcond_Wkv': 6.837,
     'L2_xcond_Wp': 5.278,
     'L3_xcond_kv_w': 8.0,
     'L3_xcond_cross_o_w': 7.909}
    for name, (base, spread) in spreads.items():
        noise = np.random.default_rng([zlib.crc32(name.encode()), seed]).standard_normal(out[name].shape)
        drawn = base * np.exp(spread * noise) if base else spread * noise
        out[name] = jnp.asarray(drawn.astype(out[name].dtype))
    for name, factor in factors.items():
        out[name] = (out[name] * factor).astype(out[name].dtype)
    return out
```

```python
import numpy as np

import concourse.bass as bass
from concourse import mybir
from contextlib import ExitStack

f32, bf16, u8 = mybir.dt.float32, mybir.dt.bfloat16, mybir.dt.uint8
ALU, ACT, AX = mybir.AluOpType, mybir.ActivationFunctionType, mybir.AxisListType

B, L, C, H, D, LC = 4, 512, 128, 16, 8, 77
PT = 128
NT = L // PT
G = 4
ITEMS = B * (H // G)
COMBOS = 6
KR = D * COMBOS
MASK0 = KR + 3
SCALE = float(np.float32(1.0) / np.sqrt(np.float32(D)))
NEG = -float(2 ** 100)
LOW = -3.0e38
SHIFT = 32
WIN = 64

ADA = [("L0_xcond_adaLN_W", 9), ("L1_xcond_w_ada", 9), ("L2_xcond_Wss_q", 2), ("L2_xcond_Wss_kv", 2),
       ("L3_xcond_ada_w", 6)]
WTS = [("L0_xcond_qkv_W", 3), ("L0_xcond_attn_out_W", 1), ("L0_xcond_cq_W", 1), ("L0_xcond_ck_W", 1),
       ("L0_xcond_cv_W", 1), ("L0_xcond_co_W", 1), ("L0_xcond_mlp_W1", 4), ("L0_xcond_mlp_W2", 4),
       ("L1_xcond_w_qkv", 3), ("L1_xcond_w_so", 1), ("L1_xcond_w_q", 1), ("L1_xcond_w_kv", 2),
       ("L1_xcond_w_co", 1), ("L1_xcond_w_m1", 8), ("L1_xcond_w_m2", 4),
       ("L2_xcond_Wq", 1), ("L2_xcond_Wkv", 2), ("L2_xcond_Wp", 1),
       ("L3_xcond_qkv_w", 3), ("L3_xcond_self_o_w", 1), ("L3_xcond_q_w", 1), ("L3_xcond_kv_w", 2),
       ("L3_xcond_cross_o_w", 1), ("L3_xcond_mlp_w1", 4), ("L3_xcond_mlp_w2", 4)]
VECS = [("L0_xcond_adaLN_b", 9), ("L0_xcond_norm1_w", 1), ("L0_xcond_normc_w", 1), ("L0_xcond_norm2_w", 1),
        ("L0_xcond_mlp_b1", 4), ("L1_xcond_b_ada", 9), ("L1_xcond_b_qkv", 3), ("L1_xcond_b_q", 1),
        ("L1_xcond_b_kv", 2), ("L1_xcond_b_m1", 8), ("L2_xcond_bq", 1), ("L2_xcond_bkv", 2),
        ("L2_xcond_bss_q", 2), ("L2_xcond_bss_kv", 2), ("L3_xcond_ada_b", 6), ("L3_xcond_qkv_b", 3),
        ("L3_xcond_norm2_g", 1), ("L3_xcond_norm2_b", 1), ("L3_xcond_q_b", 1), ("L3_xcond_kv_b", 2),
        ("L3_xcond_mlp_b1", 4), ("cond_1024", 4)]
GATES = [("L0_xcond_adaLN_b", 2), ("L0_xcond_adaLN_b", 5), ("L0_xcond_adaLN_b", 8), ("L1_xcond_b_ada", 2),
         ("L1_xcond_b_ada", 5), ("L1_xcond_b_ada", 8), ("L3_xcond_ada_b", 2), ("L3_xcond_ada_b", 5)]
ROWS = [("L0_xcond_mlp_b2", 0), ("L1_xcond_b_qkv", 2), ("L1_xcond_b_so", 0), ("L1_xcond_b_kv", 1),
        ("L1_xcond_b_co", 0), ("L1_xcond_b_m2", 0), ("L2_xcond_bkv", 1), ("L2_xcond_bp", 0),
        ("L3_xcond_qkv_b", 2), ("L3_xcond_self_o_b", 0), ("L3_xcond_kv_b", 1), ("L3_xcond_cross_o_b", 0),
        ("L3_xcond_mlp_b2", 0)]


def starts(table):
    at, n = {}, 0
    for name, k in table:
        at[name] = n
        n += k
    return at, n


ADA_AT, N_ADA = starts(ADA)
WTS_AT, N_WTS = starts(WTS)
VEC_AT, N_VEC = starts(VECS)
N_W0 = WTS_AT["L1_xcond_w_qkv"]

PHASES = [
    dict(ln=0, proj=("L0_xcond_qkv_W", None), kv=True, att=0, rope=True),
    dict(ln=1, post=("L0_xcond_attn_out_W", None, 0), proj=("L0_xcond_cq_W", None), att=1),
    dict(ln=2, post=("L0_xcond_co_W", None, 1),
         mlp=("L0_xcond_mlp_W1", "L0_xcond_mlp_b1", "L0_xcond_mlp_W2", "L0_xcond_mlp_b2", 2, False)),
    dict(ln=3, proj=("L1_xcond_w_qkv", "L1_xcond_b_qkv"), kv=True, att=2, roll=True),
    dict(ln=4, post=("L1_xcond_w_so", "L1_xcond_b_so", 3), proj=("L1_xcond_w_q", "L1_xcond_b_q"), att=3),
    dict(ln=5, post=("L1_xcond_w_co", "L1_xcond_b_co", 4),
         mlp=("L1_xcond_w_m1", "L1_xcond_b_m1", "L1_xcond_w_m2", "L1_xcond_b_m2", 5, True)),
    dict(ln=6, proj=("L2_xcond_Wq", "L2_xcond_bq"), att=4),
    dict(ln=7, post=("L2_xcond_Wp", "L2_xcond_bp", None), proj=("L3_xcond_qkv_w", "L3_xcond_qkv_b"), kv=True,
         att=5),
    dict(ln=8, post=("L3_xcond_self_o_w", "L3_xcond_self_o_b", 6), proj=("L3_xcond_q_w", "L3_xcond_q_b"),
         att=6),
    dict(ln=9, post=("L3_xcond_cross_o_w", "L3_xcond_cross_o_b", None),
         mlp=("L3_xcond_mlp_w1", "L3_xcond_mlp_b1", "L3_xcond_mlp_w2", "L3_xcond_mlp_b2", 7, False)),
]
EPS = [1e-5, 1e-5, 1e-5, 1e-6, 1e-6, 1e-6, 1e-5, 1e-6, 1e-6, 1e-6]
LN_KV = 10
SELF, WINDOW, CROSS = "self", "window", "cross"
ATTS = [dict(kind=SELF, mask=True), dict(kind=CROSS, kc=0, mask=True), dict(kind=WINDOW),
        dict(kind=CROSS, kc=1, topk=True), dict(kind=CROSS, kc=2), dict(kind=SELF), dict(kind=CROSS, kc=3)]
CONTEXT = [("L0_xcond_ck_W", 0, "L0_xcond_cv_W", 0, None, None),
           ("L1_xcond_w_kv", 0, "L1_xcond_w_kv", 1, "L1_xcond_b_kv", "L1_xcond_b_kv"),
           ("L2_xcond_Wkv", 0, "L2_xcond_Wkv", 1, "L2_xcond_bkv", "L2_xcond_bkv"),
           ("L3_xcond_kv_w", 0, "L3_xcond_kv_w", 1, "L3_xcond_kv_b", "L3_xcond_kv_b")]
BIAS = 64

for a in ATTS:
    a["KT"] = NT if a["kind"] == SELF else 1
    a["KP"] = LC if a["kind"] == CROSS else PT
    a["CM"] = NT * G if a["kind"] == SELF else 4
    a["LA"] = 2 if a["kind"] == SELF else 3
chunks = units = loads = 0
for k, a in enumerate(ATTS):
    a["k"], a["item0"], a["m0"], a["u0"] = k, BIAS + ITEMS * k, BIAS + chunks, BIAS + units
    a["t0"] = BIAS + 2 * units
    a["selfs"] = sum(x["kind"] == SELF for x in ATTS[:k])
    own = 16 if a["kind"] == CROSS and a.get("mask") else 0
    a["ldn"] = (48 if a["kind"] == SELF else 32) + own
    a["ld0"] = loads + 48 + own
    loads += 48 + own + (B - 1) * a["ldn"]
    a["mask_rows"] = {0: 32, 2: 48, 3: 64}.get(k, 0)
    chunks += ITEMS * a["CM"]
    units += ITEMS * a["KT"]


def with_(key):
    return [p for p, ph in enumerate(PHASES) if ph.get(key)]


STEP = {"ln": list(range(len(PHASES))), "post": with_("post"), "q": with_("proj"), "kv": with_("kv"),
        "mlp": with_("mlp")}


def nth(step, p, s):
    return B * STEP[step].index(p) + s + 1


def mlp_chunks(p):
    return 2 * NT if PHASES[p]["mlp"][5] else NT


def nth_chunk(p, s, c):
    return sum(B * mlp_chunks(x) for x in STEP["mlp"] if x < p) + s * mlp_chunks(p) + c + 1


def parts_written(p, s):
    return sum(16 * (6 if PHASES[x].get("kv") else 3) for x in STEP["q"] if x <= p)


def build(nc, x, ctx_in, mask_kv, mask_ss, ada, wts, vecs, gate_rows, bias_rows, rope, ident_in, side_in, out):
    stack = ExitStack()
    with stack:
        def sb(name, shape, dt=f32):
            return stack.enter_context(nc.sbuf_tensor(name, shape, dt))

        def sem(name):
            return stack.enter_context(nc.semaphore(name))

        q_scr = nc.dram_tensor("q_scr", (B, C, COMBOS, L), bf16, kind="Internal").ap()
        k_scr = nc.dram_tensor("k_scr", (B, C, COMBOS, L), bf16, kind="Internal").ap()
        c_scr = nc.dram_tensor("c_scr", (len(CONTEXT), B, C, COMBOS, LC), bf16, kind="Internal").ap()
        q_rows = q_scr.rearrange("b (g h d) s t -> (b g) (d s) h t", g=G, h=G)
        k_rows = k_scr.rearrange("b (g h d) s t -> (b g) (d s) h t", g=G, h=G)
        c_rows = [c_scr[l].rearrange("b (g h d) s t -> (b g) (d s) h t", g=G, h=G) for l in range(len(CONTEXT))]

        X = sb("X", [PT, B, NT, C])
        W = sb("W", [C, N_WTS, C])
        COL = sb("COL", [C, N_VEC])
        BROW = sb("BROW", [1, len(ROWS), C])
        ONES = sb("ONES", [1, PT])
        GATE = sb("GATE", [PT, len(GATES), B, C])
        SCSH = sb("SCSH", [C, 2, 11, B])
        IDF = sb("IDF", [PT, PT])
        IDB = sb("IDB", [PT, PT], bf16)
        IDNEG = sb("IDNEG", [PT, PT], bf16)
        SIDE = sb("SIDE", [4, L], bf16)
        SELM = sb("SELM", [PT, G, PT], bf16)
        MROW = sb("MROW", [2, B, LC], bf16)
        WROT = sb("WROT", [C, 2, C])
        QS = sb("QS", [PT, 4, G, L], bf16)
        KS = sb("KS", [PT, 4, G, L], bf16)
        ZERO = sb("ZERO", [3, L], bf16)
        P = sb("P", [PT, 2, G, L])
        UT = P
        V = sb("V", [PT, B, NT, H, D + 1])
        VC = sb("VC", [LC, len(CONTEXT), B, H, D + 1])
        VG = sb("VG", [PT, 4, NT, G, 32])
        OTS = sb("OTS", [PT, 2, L])
        ON = sb("ON", [PT, B, NT, C])
        SHARE = sb("SHARE", [PT, 6144], bf16)
        COS = SHARE[:, 0:1024].bitcast(f32)
        SIN = SHARE[:, 1024:2048].bitcast(f32)
        MASKN = SHARE[:, 2048:4096].rearrange("p (t k) -> p t k", t=NT)
        MASKT = SHARE[:, 4096:6144].rearrange("p (t k) -> p t k", t=NT)
        REST = SHARE[:, 0:4 * NT * G * LC].rearrange("p (u t h k) -> p u t h k", u=4, t=NT, h=G)
        XN = sb("XN", [PT, 2, NT, C])
        HT = sb("HT", [C, 2, L + SHIFT])
        OT_ = sb("OT_", [C, 2, L])
        TMP = sb("TMP", [PT, NT, C])
        RA = sb("RA", [C, 2, L])
        PARTS = sb("PARTS", [C, 2, 2, 3, L], bf16)
        V8 = sb("V8", [PT, 4, NT, G, 8])
        V8B = sb("V8B", [PT, 2, G, 8])
        TK = sb("TK", [PT, NT, G, LC])
        JUNK = sb("JUNK", [PT, 2, L], bf16)
        MRES = sb("MRES", [PT, 2, NT, G])
        MP = sb("MP", [PT, 4, NT, G, 3], bf16)
        MTS = sb("MTS", [PT, 4, L], bf16)
        RC = sb("RC", [PT, 2, NT, G])
        STAT = sb("STAT", [PT, NT, 6])
        MV = sb("MV", [PT, NT, 2])
        VE = sb("VE", [PT, NT])
        RSTD = sb("RSTD", [PT, 2, NT])
        HALF = sb("HALF", [PT, NT])
        COND = sb("COND", [C, 3, B])
        PF = P[:, :, :, :].rearrange("p a b c -> p (a b c)")
        ADAW = PF[:, 0:N_WTS * 0 + 28 * C].rearrange("p (n c) -> p n c", c=C)
        CTX = OTS[0:LC, 0, :].rearrange("p (b c) -> p b c", b=B)
        CTN = OTS[0:LC, 1, :].rearrange("p (b c) -> p b c", b=B)
        CXT = RA[:, 0, 0:B * LC]
        CZT = RA[:, 1, 0:B * LC]
        CREST = TMP[:, :, :].rearrange("p a b -> p (a b)")[:, 0:B * LC]
        CREP = ON[:, 0:2, :, :]
        VROW = XN[:, 0, 0, :]
        GROW = XN[0:1, 1, :, :].rearrange("p a b -> p (a b)")
        MSKU = ON[:, 2, :, :].rearrange("p a b -> p (a b)").bitcast(u8).rearrange("p (t k) -> p t k", t=NT)
        MKU = ON[0:2, 3, 0, :].bitcast(u8)[:, 0:B * LC]
        GROWS = HT[0:1, :, :].rearrange("p a b -> p (a b)")[:, 0:len(GATES) * C].rearrange("p (n c) -> p n c", c=C)

        bank = [stack.enter_context(nc.psum_tensor(f"bank{i}", [PT, 512], f32)) for i in range(2)]
        ST = [stack.enter_context(nc.psum_tensor(f"scoresT{i}", [PT, 2, 512], f32)) for i in range(2)]
        b6 = stack.enter_context(nc.psum_tensor("bank6", [PT, 512], f32))
        b7 = stack.enter_context(nc.psum_tensor("bank7", [PT, 512], f32))
        bk = [bank[0][:, :], bank[1][:, :], ST[0][:, 0, :], ST[0][:, 1, :], ST[1][:, 0, :], ST[1][:, 1, :],
              b6[:, :], b7[:, :]]

        ld_vec, ld_id, ld_ada, ld_grow, ld_brow, ld_w0, ld_w1, ld_rope, ld_mask, ld_ctx, ld_side = (
            sem(f"ld_{n}") for n in ("vec", "id", "ada", "grow", "brow", "w0", "w1", "rope", "mask", "ctx", "side"))
        ld_x = [sem(f"ld_x{s}") for s in range(B)]
        consts, set_pe, set_act, set_dve, set_pool = (
            sem(n) for n in ("consts", "set_pe", "set_act", "set_dve", "set_pool"))
        ctx_k_dma = [sem(f"ctx_k_dma{l}") for l in range(len(CONTEXT))]
        dve_step, pool_step = sem("dve_step"), sem("pool_step")
        on_turned, ot_ready, out_done, post_added = (sem(n) for n in ("on_turned", "ot_ready", "out_done", "post_added"))
        stats_ready, rstd_ready, xn_ready, xn_turned, h_ready = (
            sem(n) for n in ("stats_ready", "rstd_ready", "xn_ready", "xn_turned", "h_ready"))
        proj_q, proj_k, proj_v, v_ready = (sem(n) for n in ("proj_q", "proj_k", "proj_v", "v_ready"))
        q_roped = sem("q_roped")
        part1 = [sem("q_part1"), sem("k_part1")]
        rest1 = [sem("q_rest1"), sem("k_rest1")]
        part2 = [sem("q_part2"), sem("k_part2")]
        part3 = [sem("q_part3"), sem("k_part3")]
        scratch_written = [sem(f"scratch_written{s}") for s in range(B)]
        up_done, act_done, glu_done, down_done, mlp_added = (
            sem(n) for n in ("up_done", "act_done", "glu_done", "down_done", "mlp_added"))
        stored = sem("stored")
        m_scored, m_reduced, max_split, max_turned, max_copied = (
            sem(n) for n in ("m_scored", "m_reduced", "max_split", "max_turned", "max_copied"))
        t_scored, exp_done, vg_ready, pv_done, ot_copied, o_turned, o_inverted, o_normed = (
            sem(n) for n in ("t_scored", "exp_done", "vg_ready", "pv_done", "ot_copied", "o_turned", "o_inverted",
                             "o_normed"))
        loaded = [sem(f"loaded{u}") for u in range(4)]
        mask_rows = sem("mask_rows")
        max_rows = [sem(f"max_rows{u}") for u in range(4)]
        top_found, top_read, rest_marked = sem("top_found"), sem("top_read"), sem("rest_marked")
        pool_gate, dve_gate = sem("pool_gate"), sem("dve_gate")

        def wt(name, chunk=0):
            return W[:, WTS_AT[name] + chunk, :]

        def col(name, chunk=0):
            i = VEC_AT[name] + chunk
            return COL[:, i:i + 1]

        def brow(name, chunk=0):
            return BROW[0:1, ROWS.index((name, chunk)), :]

        def w_ready(eng, name):
            eng.wait_ge(ld_w0 if WTS_AT[name] < N_W0 else ld_w1, 16)

        def items(eng, body):
            with eng.Fori(0, B - 1) as it:
                for u in range(G):
                    body(it, u, False)
            for u in range(G):
                body(B - 1, u, True)

        def att_over(eng, k, *sems):
            a = ATTS[k]
            for s in sems:
                if s is exp_done:
                    eng.wait_ge(exp_done, a["t0"] + 2 * ITEMS * a["KT"])
                elif s is o_normed:
                    eng.wait_ge(o_normed, a["item0"] + ITEMS)
                elif s is m_reduced:
                    eng.wait_ge(m_reduced, a["m0"] + ITEMS * a["CM"])
                elif s is pv_done:
                    eng.wait_ge(pv_done, a["u0"] + ITEMS * a["KT"])
                elif s is o_turned:
                    eng.wait_ge(o_turned, a["item0"] + ITEMS)

        def h_last_read(eng, p, s):
            if "mlp" in PHASES[p]:
                eng.wait_ge(up_done, nth_chunk(p, s, mlp_chunks(p) - 1))
            elif PHASES[p].get("kv"):
                eng.wait_ge(proj_v, nth("kv", p, s))
            else:
                eng.wait_ge(proj_q, nth("q", p, s))

        def att_of(p):
            return PHASES[p - 1].get("att") if p else None

        block = stack.enter_context(nc.Block())

        @block.sync
        def _(sp):
            sp.dma_start(VROW[0:N_VEC, :], vecs).then_inc(ld_vec, 16)
            sp.dma_start(IDF[:, :], ident_in).then_inc(ld_id, 16)
            sp.dma_start(X[:, 0, :, :], x[0].rearrange("(t p) c -> p t c", p=PT)).then_inc(ld_x[0], 16)
            sp.dma_start(ADAW, ada).then_inc(ld_ada, 16)
            sp.dma_start(GROWS, gate_rows).then_inc(ld_grow, 16)
            sp.dma_start(W[:, 0:N_W0, :], wts[:, 0:N_W0, :]).then_inc(ld_w0, 16)
            sp.dma_start(CTX, ctx_in.rearrange("b k c -> k b c")).then_inc(ld_ctx, 16)
            sp.dma_start(BROW[0:1, :, :], bias_rows).then_inc(ld_brow, 16)
            for s in range(1, B):
                sp.dma_start(X[:, s, :, :], x[s].rearrange("(t p) c -> p t c", p=PT)).then_inc(ld_x[s], 16)
            sp.dma_start(SHARE[:, 0:2048].bitcast(f32), rope).then_inc(ld_rope, 16)
            sp.dma_start(MSKU, mask_ss.rearrange("(t p) k -> p t k", p=PT)).then_inc(ld_mask, 16)
            sp.dma_start(MKU, mask_kv.rearrange("b k -> (b k)")[None, :].broadcast_to([2, B * LC])
                         ).then_inc(ld_mask, 16)
            sp.dma_start(TMP[0:4, :, :].rearrange("p a b -> p (a b)"), side_in).then_inc(ld_side, 16)
            sp.dma_start(W[:, N_W0:N_WTS, :], wts[:, N_W0:N_WTS, :]).then_inc(ld_w1, 16)

            RUNS = {0: [(0, 3, None), (3, 2, None), (5, 1, None)],
                    1: [(0, 3, 0), (3, 2, 1), (5, 1, 2)]}

            def write_parts(dst, parts, side, done):
                for first, n, one in RUNS[side]:
                    src = parts[:, 0:n] if one is None else parts[:, one:one + 1].broadcast_to(
                        [C, n] + list(parts.shape[2:]))
                    sp.dma_start(dst[:, first:first + n], src).then_inc(done, 16)

            def context_parts(l):
                sp.wait_ge(set_dve, CTX_K_DVE[l])
                sp_parts = PARTS[:, 0, l % 2, :, 0:B * LC].rearrange("c s (b k) -> c s b k", b=B)
                for first, n, one in RUNS[1]:
                    for b in range(B):
                        sp.dma_start(c_scr[l, b, :, first:first + n, :],
                                     sp_parts[:, one:one + 1, b, :].broadcast_to([C, n, LC])
                                     ).then_inc(ctx_k_dma[l], 16)

            for l in range(len(CONTEXT)):
                context_parts(l)

            def phase(p):
                ph = PHASES[p]
                for s in range(B):
                    if not ph.get("proj"):
                        continue
                    for side in range(2 if ph.get("kv") else 1):
                        sp.wait_ge(part3[side], nth("kv" if side else "q", p, s))
                        write_parts((k_scr if side else q_scr)[s], PARTS[:, s % 2, side], side, scratch_written[s])

            def load(a, it, u, zero):
                item = bass.ds(it * G + u, 1)
                keys = L if a["kind"] != CROSS else LC
                rows = k_rows if a["kind"] != CROSS else c_rows[a["kc"]]
                sp.dma_start(QS[0:KR, u, :, :], q_rows[item].rearrange("o r h t -> r (o h) t")).then_inc(loaded[u], 16)
                sp.dma_start(KS[0:KR, u, :, 0:keys],
                             rows[item].rearrange("o r h t -> r (o h) t")).then_inc(loaded[u], 16)
                if a["kind"] == CROSS and a.get("mask"):
                    sp.dma_start(KS[MASK0:MASK0 + 2, u, :, 0:LC],
                                 MROW[:, bass.ds(it, 1), :].broadcast_to([2, G, LC])).then_inc(loaded[u], 16)
                if zero:
                    sp.dma_start(QS[KR:KR + 3, u, :, :], ZERO[:, None, :].broadcast_to([3, G, L])).then_inc(loaded[u], 16)

            def attention(a, p):
                sp.wait_ge(scratch_written[0], parts_written(p, 0))
                if a["k"]:
                    sp.wait_ge(t_scored, a["t0"])
                else:
                    sp.wait_ge(consts, N_CONSTS)
                if a["kind"] == CROSS:
                    sp.wait_ge(ctx_k_dma[a["kc"]], 16 * 3 * B)
                if a["k"] == 0:
                    sp.dma_start(QS[MASK0:MASK0 + 2, :, :, :].rearrange("p u h t -> p (u h) t"),
                                 SIDE[0:2, None, :].broadcast_to([2, 4 * G, L])).then_inc(mask_rows, 16)
                if a["mask_rows"]:
                    rows = ZERO[0:2, :] if a["kind"] != WINDOW else SIDE[2:4, :]
                    sp.dma_start(KS[MASK0:MASK0 + 2, :, :, :].rearrange("p u h t -> p (u h) t"),
                                 rows[:, None, :].broadcast_to([2, 4 * G, L])).then_inc(mask_rows, 16)
                for u in range(G):
                    load(a, 0, u, True)
                for s in range(1, B):
                    sp.wait_ge(scratch_written[s], parts_written(p, s))

                def max_to_q(it, u):
                    it, u = (it, u) if u < G else (it + 1, u - G)
                    sp.wait_ge(max_copied, it * G + (a["item0"] + u + 1))
                    for h in range(G):
                        sp.dma_start(QS[KR:KR + 3, u, h, :], MTS[3 * h:3 * h + 3, u, :]).then_inc(max_rows[u], 16)

                def step(it, u, last):
                    if a["kind"] == SELF and not (last and u == G - 1):
                        max_to_q(it, u + 1)
                    if not last:
                        sp.wait_ge(t_scored, it * (2 * G * a["KT"]) + (a["t0"] + 2 * a["KT"] * (u + 1)))
                        load(a, it + 1, u, a["kind"] == SELF)

                if a["kind"] == SELF:
                    max_to_q(0, 0)
                items(sp, step)

            for p in range(len(PHASES)):
                phase(p)
                if "att" in PHASES[p]:
                    attention(ATTS[PHASES[p]["att"]], p)
            last = len(PHASES) - 1
            for s in range(B):
                sp.wait_ge(mlp_added, nth("mlp", last, s))
                sp.dma_start(out[s].rearrange("(t p) c -> p t c", p=PT), X[:, s, :, :]).then_inc(stored, 16)
            sp.wait_ge(stored, 16 * B)

        @block.tensor
        def _(pe):
            pe.wait_ge(ld_vec, 16)
            pe.wait_ge(ld_id, 16)
            pe.transpose(bk[0][:, 0:N_VEC], VROW[0:N_VEC, :], IDF[0:N_VEC, 0:N_VEC]).then_inc(set_pe, 1)
            pe.wait_ge(ld_ada, 16)
            pe.wait_ge(set_dve, DVE_COND)
            for n in range(N_ADA):
                raw = n < ADA_AT["L1_xcond_w_ada"]
                mm = pe.matmul(bk[1][:, n * B:n * B + B], ADAW[:, n, :], COND[:, 0 if raw else 2, :],
                               start=True, stop=True)
            mm.then_inc(set_pe, 1)
            pe.wait_ge(set_dve, DVE_REP)
            pe.wait_ge(consts, 1)
            pe.wait_ge(ld_grow, 16)
            for n, (name, chunk) in enumerate(GATES):
                adaname = {"L0_xcond_adaLN_b": "L0_xcond_adaLN_W", "L1_xcond_b_ada": "L1_xcond_w_ada",
                           "L3_xcond_ada_b": "L3_xcond_ada_w"}[name]
                if n >= 4:
                    pe.wait_ge(set_act, ACT_GATE + n - 4 + 1)
                for b in range(B):
                    o = bk[2 + n % 4][:, b * C:b * C + C]
                    pe.matmul(o, ONES[0:1, 0:PT], GROWS[:, n, :], start=True, stop=False)
                    mm = pe.matmul(o, CREP[:, 0 if n < 3 else 1, b, :], ADAW[:, ADA_AT[adaname] + chunk, :],
                                   start=False, stop=True)
                mm.then_inc(set_pe, 1)
            pe.wait_ge(set_dve, DVE_MASK)
            for kt in range(NT):
                if kt >= 2:
                    pe.wait_ge(set_act, ACT_MASK + kt - 1)
                for qt in range(NT):
                    mm = pe.transpose(bk[6 + kt % 2].bitcast(bf16)[:, qt * PT:qt * PT + PT],
                                      MASKN[:, qt, kt * PT:kt * PT + PT], IDB[:, :])
                mm.then_inc(set_pe, 1)
            pe.wait_ge(ld_ctx, 16)
            pe.wait_ge(set_act, ACT_GATE + 8)
            for b in range(B):
                mm = pe.transpose(bk[2][:, b * LC:b * LC + LC], CTX[:, b, :], IDF[0:LC, 0:LC])
            mm.then_inc(set_pe, 1)
            pe.wait_ge(set_dve, DVE_CTXN)
            for b in range(B):
                mm = pe.transpose(bk[3][:, b * LC:b * LC + LC], CTN[:, b, :], IDF[0:LC, 0:LC])
            mm.then_inc(set_pe, 1)
            pe.wait_ge(set_act, ACT_CTX + 2)
            pe.wait_ge(ld_brow, 16)
            for l, (kw, kc, vw, vc, kb, vb) in enumerate(CONTEXT):
                w_ready(pe, kw)
                src = CZT if l == 2 else CXT
                if l >= 1:
                    pe.wait_ge(set_dve, CTX_K_DVE[l - 1] - 1)
                    pe.wait_ge(set_act, CTX_V_ACT[l - 1])
                pe.matmul(bk[4][:, 0:B * LC], wt(kw, kc), src, start=True, stop=True).then_inc(set_pe, 1)
                for b in range(B):
                    o = bk[5][0:LC, b * C:b * C + C]
                    if vb:
                        pe.matmul(o, ONES[0:1, 0:LC], brow(vb, 1), start=True, stop=False)
                    mm = pe.matmul(o, src[:, b * LC:b * LC + LC], wt(vw, vc), start=not vb, stop=True)
                mm.then_inc(set_pe, 1)
            pe.wait_ge(set_dve, CTX_K_DVE[-1])
            pe.wait_ge(set_act, CTX_V_ACT[-1])
            pe.wait_ge(consts, N_CONSTS)

            def entry(p):
                k = att_of(p)
                if k is not None:
                    att_over(pe, k, m_reduced, exp_done, o_normed)
                elif p:
                    pe.wait_ge(mlp_added, nth("mlp", p - 1, B - 1))

            def post(p, s):
                name, bias, _ = PHASES[p]["post"]
                if s >= 1:
                    pe.wait_ge(ot_ready, nth("post", p, s - 1))
                for t in range(NT):
                    mm = pe.transpose(bk[0][:, t * PT:t * PT + PT], ON[:, s, t, :], IDF[:, :])
                mm.then_inc(on_turned, 1)
                w_ready(pe, name)
                pe.wait_ge(ot_ready, nth("post", p, s))
                if s >= 1:
                    pe.wait_ge(post_added, nth("post", p, s - 1))
                for t in range(NT):
                    o = bk[1][:, t * C:t * C + C]
                    if bias:
                        pe.matmul(o, ONES[0:1, 0:PT], brow(bias), start=True, stop=False)
                    mm = pe.matmul(o, OT_[:, s % 2, t * PT:t * PT + PT], wt(name), start=not bias, stop=True)
                mm.then_inc(out_done, 1)

            def turn_xn(p, s):
                pe.wait_ge(xn_ready, nth("ln", p, s))
                if s >= 1:
                    pe.wait_ge(h_ready, nth("ln", p, s - 1))
                for t in range(NT):
                    mm = pe.transpose(bk[2][:, t * PT:t * PT + PT], XN[:, s % 2, t, :], IDF[:, :])
                mm.then_inc(xn_turned, 1)
                pe.wait_ge(h_ready, nth("ln", p, s))

            def project(p, s):
                ph = PHASES[p]
                name, bias = ph["proj"]
                w_ready(pe, name)
                off = SHIFT if ph.get("roll") else 0
                h = HT[:, s % 2, off:off + L]
                if s >= 1:
                    pe.wait_ge(rest1[0], nth("q", p, s - 1))
                mm = pe.matmul(bk[3], wt(name, 0), h, start=True, stop=True)
                if ph.get("rope"):
                    pe.wait_ge(set_dve, DVE_ROT)
                    mm = pe.matmul(bk[4], WROT[:, 0, :], h, start=True, stop=True)
                mm.then_inc(proj_q, 1)
                if not ph.get("kv"):
                    return
                if s >= 1:
                    pe.wait_ge(rest1[1], nth("kv", p, s - 1))
                mm = pe.matmul(bk[5], wt(name, 1), h, start=True, stop=True)
                if ph.get("rope"):
                    mm = pe.matmul(bk[6], WROT[:, 1, :], h, start=True, stop=True)
                mm.then_inc(proj_k, 1)
                if s >= 1:
                    pe.wait_ge(v_ready, nth("kv", p, s - 1))
                for t in range(NT):
                    o = bk[7][:, t * C:t * C + C]
                    if bias:
                        pe.matmul(o, ONES[0:1, 0:PT], brow(bias, 2), start=True, stop=False)
                    mm = pe.matmul(o, h[:, t * PT:t * PT + PT], wt(name, 2), start=not bias, stop=True)
                mm.then_inc(proj_v, 1)

            def mlp(p, s):
                w1, _, w2, b2, _, glu = PHASES[p]["mlp"]
                w_ready(pe, w2)
                h = HT[:, s % 2, 0:L]
                n = mlp_chunks(p)
                order = [c for j in range(NT) for c in ((j, NT + j) if glu else (j,))]
                for i, c in enumerate(order):
                    before = s * mlp_chunks(p) + i - 4
                    if before >= 0 and glu and before % 2:
                        pe.wait_ge(glu_done, before // 2 + 1)
                    elif before >= 0:
                        pe.wait_ge(act_done, ACT_FROM[p] + (before // 2 if glu else before) + 1)
                    pe.matmul(bk[3 + i % 4], wt(w1, c), h, start=True, stop=True).then_inc(up_done, 1)
                if s:
                    pe.wait_ge(mlp_added, nth("mlp", p, s - 1))
                if glu:
                    pe.wait_ge(glu_done, NT * (s + 1))
                else:
                    pe.wait_ge(act_done, ACT_FROM[p] + NT * (s + 1))
                for t in range(NT):
                    o = bk[7][:, t * C:t * C + C]
                    pe.matmul(o, ONES[0:1, 0:PT], brow(b2), start=True, stop=False)
                    for c in range(NT):
                        mm = pe.matmul(o, UT[:, s % 2, c, t * PT:t * PT + PT], wt(w2, c),
                                       start=False, stop=(c == NT - 1))
                mm.then_inc(down_done, 1)

            def phase(p):
                entry(p)
                for s in range(B + 1):
                    if s < B and "post" in PHASES[p]:
                        post(p, s)
                    if s >= 1:
                        turn_xn(p, s - 1)
                        (mlp if "mlp" in PHASES[p] else project)(p, s - 1)

            def attention(a, p):
                KT, KP, CM, LA, kind = a["KT"], a["KP"], a["CM"], a["LA"], a["kind"]
                masked, topk = a.get("mask"), a.get("topk")
                pe.wait_ge(part3[0], nth("q", p, B - 1))
                pe.wait_ge(h_ready, nth("ln", p, B - 1))
                if PHASES[p].get("kv"):
                    pe.wait_ge(part3[1], nth("kv", p, B - 1))
                    pe.wait_ge(v_ready, nth("kv", p, B - 1))
                if "post" in PHASES[p]:
                    pe.wait_ge(post_added, nth("post", p, B - 1))
                if a["mask_rows"]:
                    pe.wait_ge(mask_rows, a["mask_rows"])

                def m_scores(it, u, c):
                    it, u = (it, u) if u < G else (it + 1, u - G)
                    if c == 0:
                        pe.wait_ge(loaded[u], it * a["ldn"] + a["ld0"])
                    if topk:
                        pe.wait_ge(top_read, it * (G * CM) + (BIAS + CM * u + c - 1))
                    else:
                        pe.wait_ge(m_reduced, it * (G * CM) + (a["m0"] + CM * u + c - 1))
                    o = bank[c % 2]
                    if kind == SELF:
                        h, qt = c // NT, c % NT
                        mm = pe.matmul(o[:, :], QS[:, u, h, qt * PT:qt * PT + PT], KS[:, u, h, :],
                                       start=True, stop=True)
                    elif kind == WINDOW:
                        for t in range(NT):
                            w = slice(t * PT, t * PT + PT)
                            mm = pe.matmul(o[:, w], QS[:, u, c, w], KS[:, u, c, w], start=True, stop=True)
                    else:
                        for h in range(G):
                            oo = o[:, h * PT:h * PT + LC]
                            mm = pe.matmul(oo, QS[:, u, h, c * PT:c * PT + PT], KS[:, u, h, 0:LC],
                                           start=True, stop=True)
                    mm.then_inc(m_scored, 1)

                def turn_max(it, u):
                    it, u = (it, u) if u < G else (it + 1, u - G)
                    pe.wait_ge(max_split, it * G + (a["item0"] + u + 1))
                    for qt in range(NT):
                        mm = pe.transpose(b7[:, :].bitcast(bf16)[0:3 * G, qt * PT:qt * PT + PT],
                                          MP[:, u, qt, :, :].rearrange("p h s -> p (h s)"), IDB[:, :])
                    mm.then_inc(max_turned, 1)

                def t_scores(it, u, kt, pr):
                    it, u = (it, u) if u < G else (it + 1, u - G)
                    if kt == 0 and pr == 0:
                        if kind == SELF:
                            pe.wait_ge(max_rows[u], it * 64 + (64 * B * a["selfs"] + 64))
                        else:
                            pe.wait_ge(max_copied, it * G + (a["item0"] + u + 1))
                    pe.wait_ge(exp_done, it * (2 * G * KT) + (a["t0"] + 2 * (KT * u + kt) + pr - 1))
                    for x in range(2):
                        h = 2 * pr + x
                        o = ST[pr][0:KP, x, :]
                        if kind == SELF:
                            mm = pe.matmul(o, KS[:, u, h, kt * PT:kt * PT + PT], QS[:, u, h, :],
                                           start=True, stop=not masked)
                            if masked:
                                mm = pe.matmul(o, IDB[:, :], MASKT[:, kt, :], start=False, stop=True)
                            continue
                        pe.matmul(o, SELM[:, h, 0:KP], MTS[:, u, :], start=True, stop=False)
                        if kind == WINDOW:
                            for t in range(NT):
                                w = slice(t * PT, t * PT + PT)
                                mm = pe.matmul(o[:, w], KS[:, u, h, w], QS[:, u, h, w],
                                               start=False, stop=(t == NT - 1))
                            continue
                        mm = pe.matmul(o, KS[:, u, h, 0:LC], QS[:, u, h, :], start=False, stop=not topk)
                        if topk:
                            for qt in range(NT):
                                mm = pe.matmul(o[:, qt * PT:qt * PT + PT], REST[:, u, qt, h, :], IDNEG[:, :],
                                               start=False, stop=(qt == NT - 1))
                    mm.then_inc(t_scored, 1)

                def pv(it, u, kt):
                    n = KT * u + kt
                    pe.wait_ge(exp_done, it * (2 * G * KT) + (a["t0"] + 2 * n + 2))
                    if kt == 0:
                        pe.wait_ge(ot_copied, it * G + (a["item0"] + u))
                        pe.wait_ge(vg_ready, it * G + (a["item0"] + u + 1))
                    for t in range(NT if kind == WINDOW else 1):
                        w = slice(t * PT, t * PT + PT) if kind == WINDOW else slice(0, L)
                        for h in range(G):
                            mm = pe.matmul(b6[32 * h:32 * h + 32, w],
                                           VG[:, u, t if kind == WINDOW else kt, h, :],
                                           P[:, n % 2, h, w], start=(kt == 0), stop=(kt == KT - 1),
                                           tile_position=(0, 32 * h))
                    mm.then_inc(pv_done, 1)

                def turn_out(it, u, prior):
                    back = 1 if prior else 0
                    pe.wait_ge(ot_copied, it * G + (a["item0"] + u + 1 - back))
                    for qt in range(NT):
                        mm = pe.transpose(b7[:, qt * PT:qt * PT + PT], OTS[:, (u - back) % 2, qt * PT:qt * PT + PT],
                                          IDF[:, :])
                    mm.then_inc(o_turned, 1)

                def b7_free(it, u, maxes, outs):
                    pe.wait_ge(max_copied, it * G + (a["item0"] + u + maxes))
                    pe.wait_ge(o_normed, it * G + (a["item0"] + u + outs))

                def item(it, u, last, first=False):
                    left = G - u if last else 2 * G
                    per = CM // KT
                    for kt in range(KT):
                        def m(c):
                            if left > LA:
                                m_scores(it, u + LA, kt * per + c)

                        def t(pr):
                            if kt + 1 < KT:
                                t_scores(it, u, kt + 1, pr)
                            elif left > 1:
                                t_scores(it, u + 1, 0, pr)

                        m(0)
                        t(0)
                        m(1)
                        t(1)
                        m(2)
                        if kt == 0 and left > LA - 1:
                            b7_free(it, u, LA - 1, -1)
                            turn_max(it, u + LA - 1)
                        pv(it, u, kt)
                        m(3)
                        if kt == 0 and not first:
                            b7_free(it, u, LA if left > LA - 1 else left, -1)
                            turn_out(it, u, True)

                for u in range(LA):
                    for c in range(CM):
                        m_scores(0, u, c)
                for u in range(LA - 1):
                    if u:
                        b7_free(0, 0, u, 0)
                    turn_max(0, u)
                for pr in range(2):
                    t_scores(0, 0, 0, pr)
                with_first(pe, a, item)
                b7_free(B - 1, G, 0, -1)
                turn_out(B - 1, G, True)

            def with_first(eng, a, item):
                for u in range(G):
                    item(0, u, False, first=(u == 0))
                with eng.Fori(1, B - 1) as it:
                    for u in range(G):
                        item(it, u, False)
                for u in range(G):
                    item(B - 1, u, True)

            for p in range(len(PHASES)):
                phase(p)
                if "att" in PHASES[p]:
                    attention(ATTS[PHASES[p]["att"]], p)

        @block.scalar
        def _(act):
            ACT_ID, ACT_EXP = ACT.Identity, ACT.Exp
            for s in (exp_done, ot_copied, max_copied):
                act.sem_inc(s, BIAS)
            act.preload_act_table(ACT_EXP)
            act.wait_ge(set_pe, 1)
            act.activation(COL[:, :], bk[0][:, 0:N_VEC], ACT.Copy).then_inc(set_act, 1)
            act.wait_ge(set_act, 1)
            act.activation(COND[:, 1, :], COL[:, VEC_AT["cond_1024"]:VEC_AT["cond_1024"] + B], ACT_EXP,
                           scale=-1.0).then_inc(set_act, 1)
            for n in range(len(GATES)):
                act.wait_ge(set_pe, 2 + n + 1)
                act.activation(GATE[:, n, :, :], bk[2 + n % 4].rearrange("p (b c) -> p b c", b=B), ACT.Copy
                               ).then_inc(set_act, 1)
            for kt in range(NT):
                act.wait_ge(set_pe, 2 + 8 + kt + 1)
                act.activation(MASKT[:, kt, :], bk[6 + kt % 2].bitcast(bf16)[:, 0:L], ACT.Copy).then_inc(set_act, 1)
            act.wait_ge(set_pe, 2 + 8 + 4 + 1)
            act.activation(CXT, bk[2][:, 0:B * LC], ACT.Copy).then_inc(set_act, 1)
            act.wait_ge(set_pe, 2 + 8 + 4 + 2)
            act.wait_ge(set_dve, DVE_SCSH)
            for b in range(B):
                i = act.activation(CZT[:, b * LC:b * LC + LC], bk[3][:, b * LC:b * LC + LC], ACT_ID,
                                   scale=SCSH[:, 0, LN_KV, b:b + 1], bias=SCSH[:, 1, LN_KV, b:b + 1])
            i.then_inc(set_act, 1)
            for l, (kw, kc, vw, vc, kb, vb) in enumerate(CONTEXT):
                parts = PARTS[:, 0, l % 2, :, 0:B * LC]
                act.wait_ge(set_pe, CTX_PE + 2 * l + 1)
                if l >= 2:
                    act.wait_ge(ctx_k_dma[l - 2], 16 * 3 * B)
                act.activation(parts[:, 0], bk[4][:, 0:B * LC], ACT_ID if kb else ACT.Copy,
                               **({"bias": col(kb)} if kb else {})).then_inc(set_act, 1)
                act.wait_ge(set_pe, CTX_PE + 2 * l + 2)
                act.wait_ge(consts, N_CONSTS)
                act.activation(VC[:, l, :, :, 0:D].rearrange("p b h d -> p (b h) d"),
                               bk[5][0:LC, :].rearrange("p (h d) -> p h d", d=D), ACT.Copy).then_inc(set_act, 1)
                act.wait_ge(set_dve, CTX_K_DVE[l] - 1)
                act.activation(parts[:, 1], CREST, ACT.Copy).then_inc(set_act, 1)

            def post(p, s):
                act.wait_ge(on_turned, nth("post", p, s))
                if s >= 2:
                    act.wait_ge(out_done, nth("post", p, s - 2))
                if PHASES[p - 1].get("roll"):
                    act.activation(OT_[:, s % 2, SHIFT:L], bk[0][:, 0:L - SHIFT], ACT.Copy)
                    act.activation(OT_[:, s % 2, 0:SHIFT], bk[0][:, L - SHIFT:L], ACT.Copy).then_inc(ot_ready, 1)
                else:
                    act.activation(OT_[:, s % 2, :], bk[0], ACT.Copy).then_inc(ot_ready, 1)

            def scaled(p, s):
                ln = PHASES[p]["ln"]
                sc, sh = SCSH[:, 0, ln, s:s + 1], SCSH[:, 1, ln, s:s + 1]
                act.wait_ge(xn_turned, nth("ln", p, s))
                if p or s >= 2:
                    h_last_read(act, *((p, s - 2) if s >= 2 else (p - 1, s + 2)))
                if PHASES[p].get("roll"):
                    act.activation(HT[:, s % 2, L:L + SHIFT], bk[2][:, 0:SHIFT], ACT_ID, scale=sc, bias=sh)
                act.activation(HT[:, s % 2, 0:L], bk[2], ACT_ID, scale=sc, bias=sh).then_inc(h_ready, 1)

            def first_parts(p, s):
                ph = PHASES[p]
                bias = ph["proj"][1]
                before = prior_write(p, s)
                if p == 0 and s == 0:
                    act.wait_ge(ctx_k_dma[-2], 16 * 3 * B)
                    act.wait_ge(ctx_k_dma[-1], 16 * 3 * B)
                if before:
                    act.wait_ge(scratch_written[before[0]], before[1])
                for side in range(2 if ph.get("kv") else 1):
                    step = "kv" if side else "q"
                    if ph.get("rope"):
                        act.wait_ge(q_roped, 2 * s + side + 1)
                        src = RA[:, side, :]
                    else:
                        act.wait_ge((proj_q, proj_k)[side], nth(step, p, s))
                        src = bk[5 if side else 3]
                    act.activation(PARTS[:, s % 2, side, 0, :], src, ACT_ID if bias else ACT.Copy,
                                   **({"bias": col(bias, side)} if bias else {})).then_inc(part1[side], 1)
                if ph.get("kv"):
                    act.wait_ge(proj_v, nth("kv", p, s))
                    act.activation(V[:, s, :, :, 0:D].rearrange("p t h d -> p (t h) d"),
                                   bk[7].rearrange("p (h d) -> p h d", d=D), ACT.Copy).then_inc(v_ready, 1)
                for side in range(2 if ph.get("kv") else 1):
                    act.wait_ge(rest1[side], nth("kv" if side else "q", p, s))
                    act.activation(PARTS[:, s % 2, side, 1, :], RA[:, side, :], ACT.Copy).then_inc(part2[side], 1)

            def mlp(p, s):
                w1, b1, _, _, _, glu = PHASES[p]["mlp"]
                for j in range(NT):
                    act.wait_ge(up_done, nth_chunk(p, s, 2 * j if glu else j))
                    if s >= 2:
                        act.wait_ge(down_done, nth("mlp", p, s - 2))
                    i = 2 * j if glu else j
                    act.activation(UT[:, s % 2, j, :], bk[3 + i % 4], ACT.Silu if glu else ACT.Gelu_apprx_tanh,
                                   bias=col(b1, j)).then_inc(act_done, 1)

            def phase(p):
                for s in range(B + 1):
                    if s < B and "post" in PHASES[p]:
                        post(p, s)
                    if s >= 1:
                        scaled(p, s - 1)
                        (mlp if "mlp" in PHASES[p] else first_parts)(p, s - 1)

            def attention(a, p):
                KT, KP, LA, kind = a["KT"], a["KP"], a["LA"], a["kind"]
                act.preload_act_table(ACT_EXP)

                def exps(it, u, kt):
                    n = KT * u + kt
                    for pr in range(2):
                        act.wait_ge(t_scored, it * (2 * G * KT) + (a["t0"] + 2 * n + pr + 1))
                        act.wait_ge(pv_done, it * (G * KT) + (a["u0"] + n - 1))
                        act.activation(P[0:KP, n % 2, 2 * pr:2 * pr + 2, :], ST[pr][0:KP, :, :], ACT_EXP, scale=SCALE
                                       ).then_inc(exp_done, 1)

                def copy_max(it, u):
                    it, u = (it, u) if u < G else (it + 1, u - G)
                    act.wait_ge(max_turned, it * G + (a["item0"] + u + 1))
                    act.wait_ge(t_scored, it * (2 * G * KT) + (a["t0"] + 2 * KT * (u - 3)))
                    act.activation(MTS[0:3 * G, u, :], b7[:, :].bitcast(bf16)[0:3 * G, 0:L], ACT.Copy
                                   ).then_inc(max_copied, 1)

                def copy_out(it, u):
                    act.wait_ge(pv_done, it * (G * KT) + (a["u0"] + KT * (u + 1)))
                    act.wait_ge(o_turned, it * G + (a["item0"] + u - 1))
                    act.activation(OTS[:, u % 2, :], b6[:, :], ACT.Copy).then_inc(ot_copied, 1)

                def item(it, u, last, first=False):
                    left = G - u if last else 2 * G
                    for kt in range(KT):
                        exps(it, u, kt)
                        if kt == 0:
                            if not first:
                                copy_out(it, u - 1)
                            if left > LA - 1:
                                copy_max(it, u + LA - 1)

                for u in range(LA - 1):
                    copy_max(0, u)
                for u in range(G):
                    item(0, u, False, first=(u == 0))
                with act.Fori(1, B - 1) as it:
                    for u in range(G):
                        item(it, u, False)
                for u in range(G):
                    item(B - 1, u, True)
                copy_out(B - 1, G - 1)

            for p in range(len(PHASES)):
                phase(p)
                if "att" in PHASES[p]:
                    attention(ATTS[PHASES[p]["att"]], p)

        @block.vector
        def _(dve):
            steps = [0]

            def link(i):
                steps[0] += 1
                i.then_inc(dve_step, 1)
                dve.wait_ge(dve_step, steps[0])

            for s in (m_reduced, o_inverted, o_normed, top_found, top_read):
                dve.sem_inc(s, BIAS)
            cond = COL[:, VEC_AT["cond_1024"]:VEC_AT["cond_1024"] + B]
            dve.wait_ge(ld_id, 16)
            dve.tensor_copy(IDB[:, :], IDF[:, :])
            dve.tensor_scalar(IDNEG[:, :], IDF[:, :], NEG, None, ALU.mult)
            for tile in (QS[32:64, :, :, :], QS[64:PT, :, :, :], KS[64:PT, :, :, :]):
                dve.memset(tile.rearrange("p a b c -> p (a b c)").bitcast(f32), 0.0)
            dve.memset(VG[:, :, :, :, :], 0.0)
            dve.wait_ge(set_act, 2)
            dve.tensor_copy(COND[:, 0, :], cond)
            link(dve.tensor_scalar(COND[:, 1, :], COND[:, 1, :], 1.0, None, ALU.add))
            link(dve.reciprocal(COND[:, 1, :], COND[:, 1, :]))
            dve.tensor_tensor(COND[:, 2, :], cond, COND[:, 1, :], ALU.mult).then_inc(set_dve, 1)
            dve.wait_ge(set_dve, DVE_COND)
            dve.tensor_copy(CREP[:, 0, :, :], COND[:, 0, :][:, :, None].broadcast_to([C, B, C]))
            dve.tensor_copy(CREP[:, 1, :, :], COND[:, 2, :][:, :, None].broadcast_to([C, B, C])
                            ).then_inc(set_dve, 1)
            dve.wait_ge(ld_mask, 32)
            dve.tensor_scalar(MROW[:, :, :].rearrange("p b k -> p (b k)"), MKU, -NEG, NEG, ALU.mult,
                              ALU.add)
            dve.tensor_scalar(MASKN, MSKU, -NEG, NEG, ALU.mult, ALU.add).then_inc(set_dve, 1)
            dve.wait_ge(set_pe, 2)
            mod = bk[1].rearrange("p (n b) -> p n b", b=B)

            def put(kind, ln, ada_name, chunk, bias_name, plus=0.0):
                return dve.tensor_scalar(SCSH[:, kind, ln, :], mod[:, ADA_AT[ada_name] + chunk, :],
                                         col(bias_name, chunk), plus, ALU.add, ALU.add)

            for j, w in enumerate(("L0_xcond_norm1_w", "L0_xcond_normc_w", "L0_xcond_norm2_w")):
                put(1, j, "L0_xcond_adaLN_W", 3 * j, "L0_xcond_adaLN_b")
                link(put(0, j, "L0_xcond_adaLN_W", 3 * j + 1, "L0_xcond_adaLN_b", 1.0))
                dve.tensor_scalar(SCSH[:, 0, j, :], SCSH[:, 0, j, :], col(w), None, ALU.mult)
                put(1, 3 + j, "L1_xcond_w_ada", 3 * j, "L1_xcond_b_ada")
                put(0, 3 + j, "L1_xcond_w_ada", 3 * j + 1, "L1_xcond_b_ada", 1.0)
            for ln, ada_name, bias_name in ((6, "L2_xcond_Wss_q", "L2_xcond_bss_q"),
                                            (LN_KV, "L2_xcond_Wss_kv", "L2_xcond_bss_kv")):
                put(0, ln, ada_name, 0, bias_name, 1.0)
                put(1, ln, ada_name, 1, bias_name)
            for ln, chunk in ((7, 0), (9, 3)):
                put(1, ln, "L3_xcond_ada_w", chunk, "L3_xcond_ada_b")
                put(0, ln, "L3_xcond_ada_w", chunk + 1, "L3_xcond_ada_b", 1.0)
            dve.tensor_copy(SCSH[:, 0, 8, :], col("L3_xcond_norm2_g").broadcast_to([C, B]))
            dve.tensor_copy(SCSH[:, 1, 8, :], col("L3_xcond_norm2_b").broadcast_to([C, B])
                            ).then_inc(set_dve, 1)
            dve.wait_ge(ld_w0, 16)
            for i in range(2):
                w = wt("L0_xcond_qkv_W", i).rearrange("p (h d) -> p h d", d=D)
                r = WROT[:, i, :].rearrange("p (h d) -> p h d", d=D)
                dve.tensor_scalar(r[:, :, 0:D // 2], w[:, :, D // 2:D], -1.0, None, ALU.mult)
                last = dve.tensor_copy(r[:, :, D // 2:D], w[:, :, 0:D // 2])
            last.then_inc(set_dve, 1)
            dve.wait_ge(ld_ctx, 16)
            for b in range(B):
                i = dve.bn_stats(STAT[0:LC, b, :], CTX[:, b, :])
            link(i)
            for b in range(B):
                i = dve.bn_aggr(MV[0:LC, b, :], STAT[0:LC, b, :])
            i.then_inc(set_dve, 1)
            dve.wait_ge(set_pool, 1)
            for b in range(B):
                i = dve.tensor_scalar(CTN[:, b, :], CTX[:, b, :], MV[0:LC, b, 0:1], RSTD[0:LC, 0, b:b + 1],
                                      ALU.subtract, ALU.mult)
            i.then_inc(set_dve, 1)
            dve.wait_ge(ld_side, 16)
            dve.tensor_copy(SIDE[:, :], TMP[0:4, :, :].rearrange("p a b -> p (a b)")).then_inc(set_dve, 1)
            dve.wait_ge(set_dve, DVE_SIDE)
            for l, (kw, kc, vw, vc, kb, vb) in enumerate(CONTEXT):
                parts = PARTS[:, 0, l % 2, :, 0:B * LC]
                dve.wait_ge(set_act, CTX_ACT + 3 * l + 1)
                if l:
                    dve.wait_ge(set_dve, CTX_K_DVE[l - 1])
                if kb:
                    i = dve.scalar_tensor_tensor(out=CREST, in0=bk[4][:, 0:B * LC], scalar=col(kb), in1=parts[:, 0],
                                                 op0=ALU.add, op1=ALU.subtract)
                else:
                    i = dve.tensor_tensor(CREST, bk[4][:, 0:B * LC], parts[:, 0], ALU.subtract)
                i.then_inc(set_dve, 1)
                dve.wait_ge(set_act, CTX_ACT + 3 * l + 3)
                dve.tensor_tensor(parts[:, 2], CREST, parts[:, 1], ALU.subtract).then_inc(set_dve, 1)
            dve.wait_ge(set_dve, CTX_K_DVE[-1])

            def post(p, s):
                gate = PHASES[p]["post"][2]
                dve.wait_ge(out_done, nth("post", p, s))
                ps = bk[1].rearrange("p (t c) -> p t c", t=NT)
                if gate is None:
                    dve.tensor_tensor(X[:, s, :, :], ps, X[:, s, :, :], ALU.add).then_inc(post_added, 1)
                else:
                    link(dve.tensor_tensor(TMP[:, :, :], ps,
                                           GATE[:, gate, s, :][:, None, :].broadcast_to([PT, NT, C]), ALU.mult))
                    dve.tensor_tensor(X[:, s, :, :], TMP[:, :, :], X[:, s, :, :], ALU.add).then_inc(post_added, 1)
                dve.wait_ge(post_added, nth("post", p, s))

            def stats(p, s):
                if p == 0:
                    dve.wait_ge(ld_x[s], 16)
                if p or s:
                    dve.wait_ge(xn_ready, nth("ln", p, s) - 1)
                    dve.wait_ge(rstd_ready, nth("ln", p, s) - 1)
                for t in range(NT):
                    i = dve.bn_stats(STAT[:, t, :], X[:, s, t, :])
                link(i)
                for t in range(NT):
                    i = dve.bn_aggr(MV[:, t, :], STAT[:, t, :])
                i.then_inc(stats_ready, 1)

            def normalise(p, s):
                dve.wait_ge(rstd_ready, nth("ln", p, s))
                if p or s >= 2:
                    dve.wait_ge(xn_turned, nth("ln", p, s) - 2)
                dve.wait_ge(stats_ready, nth("ln", p, s))
                for t in range(NT):
                    i = dve.tensor_scalar(XN[:, s % 2, t, :], X[:, s, t, :], MV[:, t, 0:1], RSTD[:, s % 2, t:t + 1],
                                          ALU.subtract, ALU.mult)
                i.then_inc(xn_ready, 1)

            def rests(p, s):
                ph = PHASES[p]
                bias = ph["proj"][1]
                sides = range(2 if ph.get("kv") else 1)
                if ph.get("rope"):
                    dve.wait_ge(ld_rope, 16)
                    for side in sides:
                        dve.wait_ge((proj_q, proj_k)[side], s + 1)
                        if s:
                            dve.wait_ge(part3[side], s)
                        dve.tensor_tensor(RA[:, side, :], bk[5 if side else 3], COS, ALU.mult)
                        link(dve.tensor_tensor(TMP[:, :, :].rearrange("p a b -> p (a b)"), bk[6 if side else 4], SIN,
                                               ALU.mult))
                        dve.tensor_tensor(RA[:, side, :], RA[:, side, :], TMP[:, :, :].rearrange("p a b -> p (a b)"),
                                          ALU.add).then_inc(q_roped, 1)
                        dve.wait_ge(q_roped, 2 * s + side + 1)
                for side in sides:
                    n = nth("kv" if side else "q", p, s)
                    src = RA[:, side, :] if ph.get("rope") else bk[5 if side else 3]
                    dve.wait_ge(part1[side], n)
                    if n >= 2:
                        dve.wait_ge(part3[side], n - 1)
                    if bias:
                        i = dve.scalar_tensor_tensor(out=RA[:, side, :], in0=src, scalar=col(bias, side),
                                                     in1=PARTS[:, s % 2, side, 0, :], op0=ALU.add, op1=ALU.subtract)
                    else:
                        i = dve.tensor_tensor(RA[:, side, :], src, PARTS[:, s % 2, side, 0, :], ALU.subtract)
                    i.then_inc(rest1[side], 1)
                for side in sides:
                    dve.wait_ge(part2[side], nth("kv" if side else "q", p, s))
                    dve.tensor_tensor(PARTS[:, s % 2, side, 2, :], RA[:, side, :], PARTS[:, s % 2, side, 1, :],
                                      ALU.subtract).then_inc(part3[side], 1)

            def mlp(p, s):
                w1, b1, _, _, gate, glu = PHASES[p]["mlp"]
                if glu:
                    for j in range(NT):
                        dve.wait_ge(act_done, ACT_FROM[p] + NT * s + j + 1)
                        dve.wait_ge(up_done, nth_chunk(p, s, 2 * j + 1))
                        dve.scalar_tensor_tensor(out=UT[:, s % 2, j, :], in0=bk[3 + (2 * j + 1) % 4],
                                                 scalar=col(b1, NT + j), in1=UT[:, s % 2, j, :], op0=ALU.add,
                                                 op1=ALU.mult).then_inc(glu_done, 1)
                dve.wait_ge(down_done, nth("mlp", p, s))
                ps = bk[7].rearrange("p (t c) -> p t c", t=NT)
                link(dve.tensor_tensor(TMP[:, :, :], ps, GATE[:, gate, s, :][:, None, :].broadcast_to([PT, NT, C]),
                                       ALU.mult))
                dve.tensor_tensor(X[:, s, :, :], TMP[:, :, :], X[:, s, :, :], ALU.add).then_inc(mlp_added, 1)
                dve.wait_ge(mlp_added, nth("mlp", p, s))

            def phase(p):
                for s in range(B + 1):
                    if s < B:
                        if "post" in PHASES[p]:
                            post(p, s)
                        stats(p, s)
                        normalise(p, s)
                    if s >= 1:
                        (mlp if "mlp" in PHASES[p] else rests)(p, s - 1)

            def attention(a, p):
                KT, CM, kind = a["KT"], a["CM"], a["kind"]

                def reduce(it, u, c, first=False):
                    it, u = (it, u) if u < G else (it + 1, u - G)
                    if c == 0:
                        dve.wait_ge(max_split, it * G + (a["item0"] + u - 3))
                    if a.get("topk"):
                        top16(it, u, c, first)
                        return
                    dve.wait_ge(m_scored, it * (G * CM) + (a["m0"] + CM * u + c + 1))
                    ps = bank[c % 2]
                    if kind == SELF:
                        h, qt = c // NT, c % NT
                        o = V8[:, u, qt, h, 0:1]
                        if a.get("mask"):
                            dve.wait_ge(m_reduced, it * (G * CM) + (a["m0"] + CM * u + c - 1))
                            dve.sem_inc(dve_gate, 1)
                            i = dve.tensor_tensor_reduce(JUNK[:, c % 2, :], ps[:, :], MASKN[:, qt, :], 1.0, LOW,
                                                         ALU.add, ALU.max, o)
                        else:
                            i = dve.tensor_reduce(o, ps[:, :], AX.X, ALU.max)
                    elif kind == WINDOW:
                        i = dve.tensor_reduce(V8[:, u, :, c, 0], ps[:, :].rearrange("p (t k) -> p t k", t=NT), AX.X,
                                              ALU.max)
                    else:
                        i = dve.tensor_reduce(V8[:, u, c, :, 0], ps[:, :].rearrange("p (h k) -> p h k", h=G)[:, :, 0:LC],
                                              AX.X, ALU.max)
                    i.then_inc(m_reduced, 1)

                def top16(it, u, c, first):
                    ps = bank[c % 2][:, :].rearrange("p (h k) -> p h k", h=G)
                    dve.wait_ge(m_scored, it * (G * CM) + (a["m0"] + CM * u + c + 1))
                    dve.sem_inc(dve_gate, 1)
                    dve.wait_ge(rest_marked, it * (G * CM) + (BIAS + CM * u + c - 3))
                    dve.sem_inc(dve_gate, 1)
                    for h in range(G):
                        i = dve.max(V8[:, u, c, h, :], ps[:, h, 0:LC])
                    i.then_inc(top_found, 1)
                    n = CM * u + c
                    if not first:
                        dve.wait_ge(top_read, it * (G * CM) + (BIAS + n))
                        dve.sem_inc(dve_gate, 1)
                        for h in range(G):
                            i = dve.max(V8B[:, (c - 1) % 2, h, :], TK[:, (c - 1) % NT, h, :])
                        i.then_inc(top_found, 1)
                    dve.wait_ge(top_found, it * (2 * G * CM) + (BIAS + 2 * n + 1))
                    dve.sem_inc(dve_gate, 1)
                    for h in range(G):
                        i = dve.match_replace(TK[:, c, h, :], V8[:, u, c, h, :], ps[:, h, 0:LC], LOW)
                    i.then_inc(top_read, 1)
                    if first:
                        dve.sem_inc(top_found, 1)
                    else:
                        dve.wait_ge(top_found, it * (2 * G * CM) + (BIAS + 2 * n + 2))
                        dve.sem_inc(dve_gate, 1)
                        for h in range(G):
                            i = dve.match_replace(TK[:, (c - 1) % NT, h, :], V8B[:, (c - 1) % 2, h, :], TK[:, (c - 1) % NT, h, :],
                                                  LOW)
                        i.then_inc(m_reduced, 1)

                def top16_end():
                    dve.drain()
                    for h in range(G):
                        dve.max(V8B[:, (NT - 1) % 2, h, :], TK[:, NT - 1, h, :])
                    dve.drain()
                    for h in range(G):
                        i = dve.match_replace(TK[:, NT - 1, h, :], V8B[:, (NT - 1) % 2, h, :], TK[:, NT - 1, h, :], LOW)
                    i.then_inc(m_reduced, 1)

                def norm(it, u):
                    dve.wait_ge(o_turned, it * G + (a["item0"] + u + 1))
                    ps = b7[:, :].rearrange("p (t h d) -> p t h d", t=NT, h=G)
                    dve.reciprocal(RC[:, u % 2, :, :], ps[:, :, :, D]).then_inc(o_inverted, 1)
                    dve.wait_ge(o_inverted, it * G + (a["item0"] + u + 1))
                    b, g = (it, u) if u >= 0 else (it - 1, G - 1)
                    o = ON[:, bass.ds(b, 1), :, g * G * D:(g + 1) * G * D].rearrange(
                        "p o t (h d) -> p (o t) h d", d=D)
                    dve.tensor_tensor(o, ps[:, :, :, 0:D],
                                      RC[:, u % 2, :, :][:, :, :, None].broadcast_to([PT, NT, G, D]), ALU.mult
                                      ).then_inc(o_normed, 1)

                def item(it, u, last, first=False):
                    left = G - u if last else 2 * G
                    for kt in range(KT):
                        if left > a["LA"]:
                            for c in range(kt * CM // KT, (kt + 1) * CM // KT):
                                reduce(it, u + a["LA"], c)
                            if a.get("topk") and last:
                                top16_end()
                        if kt == 0 and not first:
                            norm(it, u - 1)

                for u in range(a["LA"]):
                    for c in range(CM):
                        reduce(0, u, c, first=(u == c == 0))
                for u in range(G):
                    item(0, u, False, first=(u == 0))
                with dve.Fori(1, B - 1) as it:
                    for u in range(G):
                        item(it, u, False)
                for u in range(G):
                    item(B - 1, u, True)
                norm(B - 1, G - 1)

            for p in range(len(PHASES)):
                phase(p)
                if "att" in PHASES[p]:
                    attention(ATTS[PHASES[p]["att"]], p)

        @block.gpsimd
        def _(pool):
            def fill(tile, value):
                pool.memset(tile, value).then_inc(consts, 1)
                pool.drain()

            fill(ONES[:, :], 1.0)
            fill(HALF[:, :], -0.5)
            fill(ZERO[:, :], 0.0)
            fill(MTS[:, :, :], 1.0)
            fill(V[:, :, :, :, :], 1.0)
            fill(VC[:, :, :, :, :], 1.0)
            fill(KS[32:64, :, :, :], -1.0)
            pool.memset(SELM[:, :, :], 0.0).then_inc(pool_step, 1)
            pool.wait_ge(pool_step, 1)
            for s in range(3):
                i = pool.affine_select(out=SELM[:, :, :], in_=SELM[:, :, :], compare_op=ALU.not_equal, fill=-1.0,
                                       base=-s, pattern=[[-3, G], [0, PT]], channel_multiplier=1).then_inc(pool_step, 1)
                pool.wait_ge(pool_step, 2 + s)
            pool.drain().then_inc(consts, 1)
            for s in (vg_ready, max_split, rest_marked):
                pool.sem_inc(s, BIAS)
            steps = [4]

            def link(i):
                steps[0] += 1
                i.then_inc(pool_step, 1)
                pool.wait_ge(pool_step, steps[0])

            def rsqrt(var, dst, tmp, half, eps):
                link(pool.tensor_scalar(tmp, var, eps, None, ALU.add))
                return pool.tensor_tensor(dst, tmp, half, ALU.pow)

            pool.wait_ge(set_dve, DVE_CSTAT)
            rsqrt(MV[0:LC, :, 1], RSTD[0:LC, 0, :], VE[0:LC, :], HALF[0:LC, :], 1e-5).then_inc(set_pool, 1)
            pool.wait_ge(set_pool, 1)
            pool.wait_ge(set_dve, DVE_CTXN)

            def phase(p):
                for s in range(B):
                    pool.wait_ge(stats_ready, nth("ln", p, s))
                    if p or s >= 2:
                        pool.wait_ge(xn_ready, nth("ln", p, s) - 2)
                    if p or s:
                        pool.wait_ge(rstd_ready, nth("ln", p, s) - 1)
                    rsqrt(MV[:, :, 1], RSTD[:, s % 2, :], VE[:, :], HALF[:, :], EPS[p]).then_inc(rstd_ready, 1)

            def attention(a, p):
                KT, KP, CM, kind = a["KT"], a["KP"], a["CM"], a["kind"]
                if PHASES[p].get("kv"):
                    pool.wait_ge(v_ready, nth("kv", p, B - 1))
                else:
                    pool.wait_ge(set_act, CTX_V_ACT[a["kc"]])

                    pool.wait_ge(pv_done, a["u0"])
                    pool.drain()
                    pool.memset(VG[64:PT, :, :, :, :], 0.0)
                    pool.drain()

                def step(it, u, last):
                    pool.wait_ge(pv_done, it * (G * KT) + (a["u0"] + KT * (u - 3)))
                    pool.sem_inc(pool_gate, 1)
                    b = bass.ds(it, 1)
                    if kind == CROSS:
                        pool.tensor_copy(VG[0:LC, u, 0, :, 0:D + 1],
                                         VC[:, a["kc"], b, u * G:u * G + G, :].rearrange("p o h d -> p (o h) d")
                                         ).then_inc(vg_ready, 1)
                    else:
                        pool.tensor_copy(VG[:, u, :, :, 0:D + 1],
                                         V[:, b, :, u * G:u * G + G, :].rearrange("p o t h d -> p (o t) h d")
                                         ).then_inc(vg_ready, 1)
                    if a.get("topk"):
                        pool.wait_ge(t_scored, it * (2 * G * KT) + (a["t0"] + 2 * KT * (u - 3)))
                        pool.sem_inc(pool_gate, 1)
                        for c in range(CM):
                            pool.wait_ge(m_reduced, it * (G * CM) + (a["m0"] + CM * u + c + 1))
                            pool.sem_inc(pool_gate, 1)
                            pool.tensor_scalar(REST[:, u, c, :, :], TK[:, c, :, :], LOW, None, ALU.is_gt
                                               ).then_inc(rest_marked, 1)
                    pool.wait_ge(m_reduced, it * (G * CM) + (a["m0"] + CM * (u + 1)))
                    pool.sem_inc(pool_gate, 1)
                    pool.wait_ge(max_turned, it * G + (a["item0"] + u - 3))
                    pool.sem_inc(pool_gate, 1)
                    mx = V8[:, u, :, :, 0]
                    pool.tensor_copy(MP[:, u, :, :, 0], mx)
                    pool.drain()
                    pool.tensor_tensor(MRES[:, 0, :, :], mx, MP[:, u, :, :, 0], ALU.subtract)
                    pool.drain()
                    pool.tensor_copy(MP[:, u, :, :, 1], MRES[:, 0, :, :])
                    pool.drain()
                    pool.tensor_tensor(MP[:, u, :, :, 2], MRES[:, 0, :, :], MP[:, u, :, :, 1], ALU.subtract
                                       ).then_inc(max_split, 1)

                with pool.Fori(0, B) as it:
                    for u in range(G):
                        step(it, u, False)

            for s in (m_scored, max_turned, t_scored, pv_done, o_turned):
                pool.sem_inc(s, BIAS)
            for p in range(len(PHASES)):
                phase(p)
                if "att" in PHASES[p]:
                    attention(ATTS[PHASES[p]["att"]], p)


DVE_COND, DVE_REP, DVE_MASK, DVE_SCSH, DVE_ROT, DVE_CSTAT, DVE_CTXN, DVE_SIDE = range(1, 9)
CTX_K_DVE = [DVE_SIDE + 2 * (l + 1) for l in range(len(CONTEXT))]
ACT_GATE = 2
ACT_MASK = ACT_GATE + len(GATES)
ACT_CTX = ACT_MASK + NT
CTX_ACT = ACT_CTX + 2
CTX_V_ACT = [CTX_ACT + 3 * l + 2 for l in range(len(CONTEXT))]
CTX_PE = 2 + len(GATES) + NT + 2
N_CONSTS = 8
ACT_FROM = {p: sum(B * NT for x in STEP["mlp"] if x < p) for p in STEP["mlp"]}


def prior_write(p, s):
    if s >= 2:
        return s - 2, parts_written(p, s - 2)
    i = STEP["q"].index(p)
    return (s + 2, parts_written(STEP["q"][i - 1], s + 2)) if i else None


def kernel(**inputs):
    import concourse.bacc as _bacc
    from concourse.bass_utils import run_bass_kernel_spmd as _run

    nc = _bacc.Bacc("TRN2", target_bir_lowering=False, num_devices=1)

    def chunked(name, n):
        w = np.asarray(inputs[name])
        return w.reshape(C, n, C) if w.shape[0] == C else w.reshape(n, C, C).transpose(1, 0, 2)

    def vec(name, chunk):
        return np.asarray(inputs[name]).reshape(-1, C)[chunk]

    d = D // 2
    freq = np.float32(1.0) / np.float32(10000.0) ** (np.arange(0, D, 2, dtype=np.float32) / D)
    angle = np.outer(np.arange(L // 2, dtype=np.float32), freq)
    angle = np.concatenate([angle, angle], axis=-1)
    table = [np.tile(fn(angle).astype(np.float32).T, (H, 2)) for fn in (np.cos, np.sin)]
    odd = (np.arange(L) // WIN % 2).astype(np.float32)
    arrays = {
        "x": np.asarray(inputs["x"]), "ctx": np.asarray(inputs["ctx_1024"]),
        "mask_kv": np.asarray(inputs["mask_BxS2_bf1"]), "mask_ss": np.asarray(inputs["mask_SxS_bk0"]),
        "ada": np.concatenate([chunked(*e) for e in ADA], axis=1),
        "wts": np.concatenate([chunked(*e) for e in WTS], axis=1),
        "vecs": np.concatenate([np.asarray(inputs[n]).reshape(-1, C) for n, _ in VECS], axis=0),
        "gate_rows": np.stack([vec(*e) for e in GATES])[None],
        "bias_rows": np.stack([vec(*e) for e in ROWS])[None],
        "rope": np.concatenate(table, axis=1),
        "ident": np.eye(PT, dtype=np.float32),
        "side": np.stack([1 - odd, odd, NEG * odd, NEG * (1 - odd)]).astype(np.float32),
    }
    arrays = {f"in_{k}": np.ascontiguousarray(v) for k, v in arrays.items()}
    args = [nc.dram_tensor(k, v.shape, mybir.dt.from_np(v.dtype), kind="ExternalInput").ap()
            for k, v in arrays.items()]
    o = nc.dram_tensor("out_0", (B, L, C), f32, kind="ExternalOutput").ap()
    build(nc, *args, o)
    return _run(nc, [arrays], core_ids=[0]).results[0]["out_0"]
```

```python
import numpy as np

import concourse.bass as bass
from concourse import mybir
from contextlib import ExitStack

f32, bf16, u8 = mybir.dt.float32, mybir.dt.bfloat16, mybir.dt.uint8
ALU, ACT, AX = mybir.AluOpType, mybir.ActivationFunctionType, mybir.AxisListType

B, L, C, H, D, LC = 4, 512, 128, 16, 8, 77
PT = 128
NT = L // PT
G = 4
ITEMS = B * (H // G)
COMBOS = 6
KR = D * COMBOS
MASK0 = KR
MAX0, MAXES = 64, 3 * 4
SCALE = float(np.float32(1.0) / np.sqrt(np.float32(D)))
NEG = -float(2 ** 100)
LOW = -3.0e38
SHIFT = 32
WIN = 64

ADA = [("L0_xcond_adaLN_W", 9), ("L1_xcond_w_ada", 9), ("L2_xcond_Wss_q", 2), ("L2_xcond_Wss_kv", 2),
       ("L3_xcond_ada_w", 6)]
WTS = [("L0_xcond_qkv_W", 3), ("L0_xcond_attn_out_W", 1), ("L0_xcond_cq_W", 1), ("L0_xcond_ck_W", 1),
       ("L0_xcond_cv_W", 1), ("L0_xcond_co_W", 1), ("L0_xcond_mlp_W1", 4), ("L0_xcond_mlp_W2", 4),
       ("L1_xcond_w_qkv", 3), ("L1_xcond_w_so", 1), ("L1_xcond_w_q", 1), ("L1_xcond_w_kv", 2),
       ("L1_xcond_w_co", 1), ("L1_xcond_w_m1", 8), ("L1_xcond_w_m2", 4),
       ("L2_xcond_Wq", 1), ("L2_xcond_Wkv", 2), ("L2_xcond_Wp", 1),
       ("L3_xcond_qkv_w", 3), ("L3_xcond_self_o_w", 1), ("L3_xcond_q_w", 1), ("L3_xcond_kv_w", 2),
       ("L3_xcond_cross_o_w", 1), ("L3_xcond_mlp_w1", 4), ("L3_xcond_mlp_w2", 4)]
VECS = [("L0_xcond_adaLN_b", 9), ("L0_xcond_norm1_w", 1), ("L0_xcond_normc_w", 1), ("L0_xcond_norm2_w", 1),
        ("L0_xcond_mlp_b1", 4), ("L1_xcond_b_ada", 9), ("L1_xcond_b_qkv", 3), ("L1_xcond_b_q", 1),
        ("L1_xcond_b_kv", 2), ("L1_xcond_b_m1", 8), ("L2_xcond_bq", 1), ("L2_xcond_bkv", 2),
        ("L2_xcond_bss_q", 2), ("L2_xcond_bss_kv", 2), ("L3_xcond_ada_b", 6), ("L3_xcond_qkv_b", 3),
        ("L3_xcond_norm2_g", 1), ("L3_xcond_norm2_b", 1), ("L3_xcond_q_b", 1), ("L3_xcond_kv_b", 2),
        ("L3_xcond_mlp_b1", 4), ("cond_1024", 4)]
GATES = [("L0_xcond_adaLN_b", 2), ("L0_xcond_adaLN_b", 5), ("L0_xcond_adaLN_b", 8), ("L1_xcond_b_ada", 2),
         ("L1_xcond_b_ada", 5), ("L1_xcond_b_ada", 8), ("L3_xcond_ada_b", 2), ("L3_xcond_ada_b", 5)]
ROWS = [("L0_xcond_mlp_b2", 0), ("L1_xcond_b_qkv", 2), ("L1_xcond_b_so", 0), ("L1_xcond_b_kv", 1),
        ("L1_xcond_b_co", 0), ("L1_xcond_b_m2", 0), ("L2_xcond_bkv", 1), ("L2_xcond_bp", 0),
        ("L3_xcond_qkv_b", 2), ("L3_xcond_self_o_b", 0), ("L3_xcond_kv_b", 1), ("L3_xcond_cross_o_b", 0),
        ("L3_xcond_mlp_b2", 0)]


def starts(table):
    at, n = {}, 0
    for name, k in table:
        at[name] = n
        n += k
    return at, n


ADA_AT, N_ADA = starts(ADA)
WTS_AT, N_WTS = starts(WTS)
VEC_AT, N_VEC = starts(VECS)
N_W0 = WTS_AT["L1_xcond_w_qkv"]

PHASES = [
    dict(ln=0, proj=("L0_xcond_qkv_W", None), kv=True, att=0, rope=True),
    dict(ln=1, post=("L0_xcond_attn_out_W", None, 0), proj=("L0_xcond_cq_W", None), att=1),
    dict(ln=2, post=("L0_xcond_co_W", None, 1),
         mlp=("L0_xcond_mlp_W1", "L0_xcond_mlp_b1", "L0_xcond_mlp_W2", "L0_xcond_mlp_b2", 2, False)),
    dict(ln=3, proj=("L1_xcond_w_qkv", "L1_xcond_b_qkv"), kv=True, att=2, roll=True),
    dict(ln=4, post=("L1_xcond_w_so", "L1_xcond_b_so", 3), proj=("L1_xcond_w_q", "L1_xcond_b_q"), att=3),
    dict(ln=5, post=("L1_xcond_w_co", "L1_xcond_b_co", 4),
         mlp=("L1_xcond_w_m1", "L1_xcond_b_m1", "L1_xcond_w_m2", "L1_xcond_b_m2", 5, True)),
    dict(ln=6, proj=("L2_xcond_Wq", "L2_xcond_bq"), att=4),
    dict(ln=7, post=("L2_xcond_Wp", "L2_xcond_bp", None), proj=("L3_xcond_qkv_w", "L3_xcond_qkv_b"), kv=True,
         att=5),
    dict(ln=8, post=("L3_xcond_self_o_w", "L3_xcond_self_o_b", 6), proj=("L3_xcond_q_w", "L3_xcond_q_b"),
         att=6),
    dict(ln=9, post=("L3_xcond_cross_o_w", "L3_xcond_cross_o_b", None),
         mlp=("L3_xcond_mlp_w1", "L3_xcond_mlp_b1", "L3_xcond_mlp_w2", "L3_xcond_mlp_b2", 7, False)),
]
EPS = [1e-5, 1e-5, 1e-5, 1e-6, 1e-6, 1e-6, 1e-5, 1e-6, 1e-6, 1e-6]
LN_KV = 10
SELF, WINDOW, CROSS = "self", "window", "cross"
ATTS = [dict(kind=SELF, mask=True), dict(kind=CROSS, kc=0, mask=True), dict(kind=WINDOW),
        dict(kind=CROSS, kc=1, topk=True), dict(kind=CROSS, kc=2), dict(kind=SELF), dict(kind=CROSS, kc=3)]
CONTEXT = [("L0_xcond_ck_W", 0, "L0_xcond_cv_W", 0, None, None),
           ("L1_xcond_w_kv", 0, "L1_xcond_w_kv", 1, "L1_xcond_b_kv", "L1_xcond_b_kv"),
           ("L2_xcond_Wkv", 0, "L2_xcond_Wkv", 1, "L2_xcond_bkv", "L2_xcond_bkv"),
           ("L3_xcond_kv_w", 0, "L3_xcond_kv_w", 1, "L3_xcond_kv_b", "L3_xcond_kv_b")]
BIAS = 64

for a in ATTS:
    a["KT"] = NT if a["kind"] == SELF else 1
    a["KP"] = LC if a["kind"] == CROSS else PT
    a["CM"] = NT * G if a["kind"] == SELF else 4
    a["LA"] = 2 if a["kind"] == SELF else 3
chunks = units = loads = 0
for k, a in enumerate(ATTS):
    a["k"], a["item0"], a["m0"], a["u0"] = k, BIAS + ITEMS * k, BIAS + chunks, BIAS + units
    a["t0"] = BIAS + 2 * units
    a["selfs"] = sum(x["kind"] == SELF for x in ATTS[:k])
    own = 16 if a["kind"] == CROSS and a.get("mask") else 0
    a["ldn"] = 32 + own
    a["ld0"] = loads + a["ldn"]
    loads += B * a["ldn"]
    a["rows_set"] = {0: 48, 1: 64, 2: 80, 3: 96, 6: 112}.get(k, 0)
    chunks += ITEMS * a["CM"]
    units += ITEMS * a["KT"]


def with_(key):
    return [p for p, ph in enumerate(PHASES) if ph.get(key)]


STEP = {"ln": list(range(len(PHASES))), "post": with_("post"), "q": with_("proj"), "kv": with_("kv"),
        "mlp": with_("mlp")}


def nth(step, p, s):
    return B * STEP[step].index(p) + s + 1


def mlp_chunks(p):
    return 2 * NT if PHASES[p]["mlp"][5] else NT


def nth_chunk(p, s, c):
    return sum(B * mlp_chunks(x) for x in STEP["mlp"] if x < p) + s * mlp_chunks(p) + c + 1


def joined(p):
    if not PHASES[p].get("post"):
        return 0
    return 2 if ATTS[PHASES[p - 1]["att"]]["kind"] == SELF else 1


def parts_written(p, s):
    return sum(16 * (6 if PHASES[x].get("kv") else 3) for x in STEP["q"] if x <= p)


def build(nc, x, ctx_in, mask_kv, mask_ss, ada, wts, vecs, bias_rows, rope, ident_in, side_in, out):
    stack = ExitStack()
    with stack:
        def sb(name, shape, dt=f32):
            return stack.enter_context(nc.sbuf_tensor(name, shape, dt))

        def sem(name):
            return stack.enter_context(nc.semaphore(name))

        q_scr = nc.dram_tensor("q_scr", (B, C, COMBOS, L), bf16, kind="Internal").ap()
        k_scr = nc.dram_tensor("k_scr", (B, C, COMBOS, L), bf16, kind="Internal").ap()
        c_scr = nc.dram_tensor("c_scr", (len(CONTEXT), C, COMBOS, B * LC), bf16, kind="Internal").ap()
        q_rows = q_scr.rearrange("b (g h d) s t -> (b g) (d s) h t", g=G, h=G)
        k_rows = k_scr.rearrange("b (g h d) s t -> (b g) (d s) h t", g=G, h=G)
        c_rows = [c_scr[l].rearrange("(g h d) s (b t) -> g (d s) h b t", g=G, h=G, b=B) for l in range(len(CONTEXT))]

        X = sb("X", [PT, B, NT, C])
        W = sb("W", [C, N_WTS, C])
        COL = sb("COL", [C, N_VEC])
        BROW = sb("BROW", [1, len(ROWS), C])
        ONES = sb("ONES", [PT, PT])
        GCOL = sb("GCOL", [C, len(GATES), B])
        GATE = sb("GATE", [PT, len(GATES), B, C])
        SCSH = sb("SCSH", [C, 2, 11, B])
        IDF = sb("IDF", [PT, PT])
        IDB = sb("IDB", [PT, PT], bf16)
        IDNEG = sb("IDNEG", [PT, PT], bf16)
        SIDE = sb("SIDE", [4, L], bf16)
        SELM = sb("SELM", [PT, G, PT], bf16)
        MROW = sb("MROW", [2, B, LC], bf16)
        WROT = sb("WROT", [C, 2, C])
        QS = sb("QS", [PT, 4, G, L], bf16)
        KS = sb("KS", [PT, 4, G, L], bf16)
        ZERO = sb("ZERO", [MAXES, L], bf16)
        P = sb("P", [PT, 2, G, L])
        UT = P
        V = sb("V", [PT, B, NT, H, D + 1])
        VC = sb("VC", [LC, len(CONTEXT), B, H, D + 1])
        VG = sb("VG", [PT, 4, NT, G, 32])
        OTS = sb("OTS", [PT, 2, L])
        ON = sb("ON", [PT, B, NT, C])
        SHARE = sb("SHARE", [PT, 6144], bf16)
        COS = SHARE[:, 0:1024].bitcast(f32)
        SIN = SHARE[:, 1024:2048].bitcast(f32)
        MASKN = SHARE[:, 2048:4096].rearrange("p (t k) -> p t k", t=NT)
        MASKT = SHARE[:, 4096:6144].rearrange("p (t k) -> p t k", t=NT)
        REST = SHARE[:, 0:4 * NT * G * LC].rearrange("p (u t h k) -> p u t h k", u=4, t=NT, h=G)
        XN = sb("XN", [PT, 2, NT, C])
        HT = sb("HT", [C, 2, L + SHIFT])
        OT_ = sb("OT_", [C, 2, L])
        TMP = sb("TMP", [PT, NT, C])
        RA = sb("RA", [C, 2, L])
        PARTS = sb("PARTS", [C, 2, 2, 3, L], bf16)
        V8 = sb("V8", [PT, 4, NT, G, 8])
        V8B = sb("V8B", [PT, 2, G, 8])
        TK = sb("TK", [PT, NT, G, LC])
        JUNK = sb("JUNK", [PT, 2, L], bf16)
        MRES = sb("MRES", [PT, 2, NT, G])
        MP = sb("MP", [PT, 4, NT, G, 3], bf16)
        MTS = sb("MTS", [PT, 4, L], bf16)
        OWN = MTS[0:MAXES, :, :].rearrange("p a b -> p (a b)")
        RC = sb("RC", [PT, 2, NT, G])
        STAT = sb("STAT", [PT, NT, 6])
        MV = sb("MV", [PT, NT, 2])
        VE = sb("VE", [PT, NT])
        RSTD = sb("RSTD", [PT, 3, NT])
        HALF = sb("HALF", [PT, NT])
        COND = sb("COND", [C, 3, B])
        PF = P[:, :, :, :].rearrange("p a b c -> p (a b c)")
        ADAW = PF[:, 0:N_WTS * 0 + 28 * C].rearrange("p (n c) -> p n c", c=C)
        CTX = OTS[0:LC, 0, :].rearrange("p (b c) -> p b c", b=B)
        CTN = OTS[0:LC, 1, :].rearrange("p (b c) -> p b c", b=B)
        TKF = TK[:, :, :, :].rearrange("p a b c -> p (a b c)")
        CXT, CZT, CREST = (TKF[:, i * B * LC:(i + 1) * B * LC] for i in range(3))
        DIAG = ON[:, 0:2, :, :]
        VROW = XN[:, 0, 0, :]
        MSKU = ON[:, 2, :, :].rearrange("p a b -> p (a b)").bitcast(u8).rearrange("p (t k) -> p t k", t=NT)
        MKU = TKF[0:2, 3 * B * LC:4 * B * LC].bitcast(u8)[:, 0:B * LC]
        SIDE32 = PF[0:4, 28 * C:28 * C + L]
        CPARTS = [t.rearrange("p a b -> p (a b)").bitcast(bf16)[:, 0:3 * B * LC].rearrange("p (s k) -> p s k", s=3)
                  for t in (JUNK[:, :, :], ON[:, 3, :, :])]


        bank = [stack.enter_context(nc.psum_tensor(f"bank{i}", [PT, 512], f32)) for i in range(2)]
        ST = [stack.enter_context(nc.psum_tensor(f"scoresT{i}", [PT, 2, 512], f32)) for i in range(2)]
        b6 = stack.enter_context(nc.psum_tensor("bank6", [PT, 512], f32))
        b7 = stack.enter_context(nc.psum_tensor("bank7", [PT, 512], f32))
        bk = [bank[0][:, :], bank[1][:, :], ST[0][:, 0, :], ST[0][:, 1, :], ST[1][:, 0, :], ST[1][:, 1, :],
              b6[:, :], b7[:, :]]

        ld_vec, ld_id, ld_ada, ld_brow, ld_w0, ld_w1, ld_rope, ld_mask, ld_ctx, ld_side = (
            sem(f"ld_{n}") for n in ("vec", "id", "ada", "brow", "w0", "w1", "rope", "mask", "ctx", "side"))
        ld_x = [sem(f"ld_x{s}") for s in range(B)]
        consts, set_pe, set_act, set_dve, set_pool = (
            sem(n) for n in ("consts", "set_pe", "set_act", "set_dve", "set_pool"))
        ctx_k_dma = [sem(f"ctx_k_dma{l}") for l in range(len(CONTEXT))]
        dve_step, pool_step = sem("dve_step"), sem("pool_step")
        on_turned, ot_ready, out_done, post_added = (sem(n) for n in ("on_turned", "ot_ready", "out_done", "post_added"))
        stats_ready, rstd_ready, xn_ready, xn_turned, h_ready = (
            sem(n) for n in ("stats_ready", "rstd_ready", "xn_ready", "xn_turned", "h_ready"))
        proj_q, proj_k, proj_v, v_ready = (sem(n) for n in ("proj_q", "proj_k", "proj_v", "v_ready"))
        q_roped = sem("q_roped")
        part1 = [sem("q_part1"), sem("k_part1")]
        rest1 = [sem("q_rest1"), sem("k_rest1")]
        part2 = [sem("q_part2"), sem("k_part2")]
        part3 = [sem("q_part3"), sem("k_part3")]
        scratch_written = [sem(f"scratch_written{s}") for s in range(B)]
        up_done, act_done, glu_done, down_done, mlp_added = (
            sem(n) for n in ("up_done", "act_done", "glu_done", "down_done", "mlp_added"))
        stored = sem("stored")
        m_scored, m_reduced, max_split, max_turned, max_copied = (
            sem(n) for n in ("m_scored", "m_reduced", "max_split", "max_turned", "max_copied"))
        t_scored, exp_done, vg_ready, pv_done, ot_copied, o_turned, o_inverted, o_normed = (
            sem(n) for n in ("t_scored", "exp_done", "vg_ready", "pv_done", "ot_copied", "o_turned", "o_inverted",
                             "o_normed"))
        loaded = [sem(f"loaded{u}") for u in range(4)]
        rows_set = sem("rows_set")
        max_rows = [sem(f"max_rows{u}") for u in range(4)]
        top_found, top_read, rest_marked = sem("top_found"), sem("top_read"), sem("rest_marked")
        pool_gate, dve_gate = sem("pool_gate"), sem("dve_gate")

        def wt(name, chunk=0):
            return W[:, WTS_AT[name] + chunk, :]

        def col(name, chunk=0):
            i = VEC_AT[name] + chunk
            return COL[:, i:i + 1]

        def brow(name, chunk=0):
            return BROW[0:1, ROWS.index((name, chunk)), :]

        def w_ready(eng, name):
            eng.wait_ge(ld_w0 if WTS_AT[name] < N_W0 else ld_w1, 16)

        def items(eng, body):
            with eng.Fori(0, B - 1) as it:
                for u in range(G):
                    body(it, u, False)
            for u in range(G):
                body(B - 1, u, True)

        def att_over(eng, k, *sems):
            a = ATTS[k]
            for s in sems:
                if s is exp_done:
                    eng.wait_ge(exp_done, a["t0"] + 2 * ITEMS * a["KT"])
                elif s is o_normed:
                    eng.wait_ge(o_normed, a["item0"] + ITEMS)
                elif s is m_reduced:
                    eng.wait_ge(m_reduced, a["m0"] + ITEMS * a["CM"])
                elif s is pv_done:
                    eng.wait_ge(pv_done, a["u0"] + ITEMS * a["KT"])
                elif s is o_turned:
                    eng.wait_ge(o_turned, a["item0"] + ITEMS)

        def h_last_read(eng, p, s):
            if "mlp" in PHASES[p]:
                eng.wait_ge(up_done, nth_chunk(p, s, mlp_chunks(p) - 1))
            elif PHASES[p].get("kv"):
                eng.wait_ge(proj_v, nth("kv", p, s))
            else:
                eng.wait_ge(proj_q, nth("q", p, s))

        def att_of(p):
            return PHASES[p - 1].get("att") if p else None

        block = stack.enter_context(nc.Block())

        @block.sync
        def _(sp):
            sp.dma_start(VROW[0:N_VEC, :], vecs).then_inc(ld_vec, 16)
            sp.dma_start(IDF[:, :], ident_in).then_inc(ld_id, 16)
            sp.dma_start(X[:, 0, :, :], x[0].rearrange("(t p) c -> p t c", p=PT)).then_inc(ld_x[0], 16)
            sp.dma_start(ADAW, ada).then_inc(ld_ada, 16)
            sp.dma_start(W[:, 0:N_W0, :], wts[:, 0:N_W0, :]).then_inc(ld_w0, 16)
            for s in range(1, B):
                sp.dma_start(X[:, s, :, :], x[s].rearrange("(t p) c -> p t c", p=PT)).then_inc(ld_x[s], 16)
            sp.dma_start(SHARE[:, 0:2048].bitcast(f32), rope).then_inc(ld_rope, 16)
            sp.dma_start(CTX, ctx_in.rearrange("b k c -> k b c")).then_inc(ld_ctx, 16)
            sp.dma_start(BROW[0:1, :, :], bias_rows).then_inc(ld_brow, 16)
            sp.dma_start(MSKU, mask_ss.rearrange("(t p) k -> p t k", p=PT)).then_inc(ld_mask, 16)
            sp.dma_start(MKU, mask_kv.rearrange("b k -> (b k)")[None, :].broadcast_to([2, B * LC])
                         ).then_inc(ld_mask, 16)
            sp.dma_start(SIDE32, side_in).then_inc(ld_side, 16)
            sp.dma_start(W[:, N_W0:N_WTS, :], wts[:, N_W0:N_WTS, :]).then_inc(ld_w1, 16)

            RUNS = {0: [(0, 3, None), (3, 2, None), (5, 1, None)],
                    1: [(0, 3, 0), (3, 2, 1), (5, 1, 2)]}

            def write_parts(dst, parts, side, done):
                for first, n, one in RUNS[side]:
                    src = parts[:, 0:n] if one is None else parts[:, one:one + 1].broadcast_to(
                        [C, n] + list(parts.shape[2:]))
                    sp.dma_start(dst[:, first:first + n], src).then_inc(done, 16)

            def context_parts(l):
                sp.wait_ge(set_dve, DVE[f"part3_{l}"])
                for first, n, one in RUNS[1]:
                    sp.dma_start(c_scr[l, :, first:first + n, :],
                                 CPARTS[l % 2][:, one:one + 1].broadcast_to([C, n, B * LC])
                                 ).then_inc(ctx_k_dma[l], 16)

            def phase(p):
                ph = PHASES[p]
                if not ph.get("proj"):
                    return
                for s in range(B):
                    if s == B - 1:
                        first_loads(ATTS[ph["att"]], p)
                    for side in range(2 if ph.get("kv") else 1):
                        sp.wait_ge(part3[side], nth("kv" if side else "q", p, s))
                        write_parts((k_scr if side else q_scr)[s], PARTS[:, s % 2, side], side, scratch_written[s])
                    if p == 0 and s:
                        context_parts(s - 1)

            def load(a, it, u):
                item = bass.ds(it * G + u, 1)
                keys = L if a["kind"] != CROSS else LC
                if a["kind"] == CROSS:
                    k_item = c_rows[a["kc"]][u, :, :, bass.ds(it, 1), :].rearrange("r h o t -> r (h o) t")
                else:
                    k_item = k_rows[item].rearrange("o r h t -> r (o h) t")
                sp.dma_start(QS[0:KR, u, :, :], q_rows[item].rearrange("o r h t -> r (o h) t")).then_inc(loaded[u], 16)
                sp.dma_start(KS[0:KR, u, :, 0:keys], k_item).then_inc(loaded[u], 16)
                if a["kind"] == CROSS and a.get("mask"):
                    sp.dma_start(KS[MASK0:MASK0 + 2, u, :, 0:LC],
                                 MROW[:, bass.ds(it, 1), :].broadcast_to([2, G, LC])).then_inc(loaded[u], 16)

            def first_loads(a, p):
                sp.wait_ge(scratch_written[0], parts_written(p, 0))
                if a["k"]:
                    sp.wait_ge(t_scored, a["t0"])
                else:
                    sp.wait_ge(consts, CONSTS["QS64"])
                if a["kind"] == CROSS:
                    sp.wait_ge(ctx_k_dma[a["kc"]], 16 * 3)
                if a["k"] == 0:
                    sp.dma_start(QS[MASK0:MASK0 + 2, :, :, :].rearrange("p u h t -> p (u h) t"),
                                 SIDE[0:2, None, :].broadcast_to([2, 4 * G, L])).then_inc(rows_set, 16)
                    sp.dma_start(KS[MAX0:MAX0 + MAXES, :, :, :].rearrange("p u h t -> p u (h t)"),
                                 OWN[:, None, :].broadcast_to([MAXES, 4, G * L])).then_inc(rows_set, 16)
                if a["k"] in (1, 6):
                    sp.dma_start(QS[MAX0:MAX0 + MAXES, :, :, :].rearrange("p u h t -> p (u h) t"),
                                 ZERO[:, None, :].broadcast_to([MAXES, 4 * G, L])).then_inc(rows_set, 16)
                elif a["rows_set"]:
                    rows = ZERO[0:2, :] if a["kind"] != WINDOW else SIDE[2:4, :]
                    sp.dma_start(KS[MASK0:MASK0 + 2, :, :, :].rearrange("p u h t -> p (u h) t"),
                                 rows[:, None, :].broadcast_to([2, 4 * G, L])).then_inc(rows_set, 16)
                for u in range(G):
                    load(a, 0, u)

            def attention(a, p):
                for s in range(1, B):
                    sp.wait_ge(scratch_written[s], parts_written(p, s))

                ahead = a["LA"] - 1

                def max_to_q(it, u):
                    it, u = (it, u) if u < G else (it + 1, u - G)
                    sp.wait_ge(max_copied, it * G + (a["item0"] + u + 1))
                    sp.dma_start(QS[MAX0:MAX0 + MAXES, u, :, :],
                                 MTS[0:MAXES, u:u + 1, :].broadcast_to([MAXES, G, L])).then_inc(max_rows[u], 16)

                def step(it, u, last):
                    more = not (last and u + ahead >= G)
                    if a["kind"] == SELF and more:
                        max_to_q(it, u + ahead)
                    if not last:
                        sp.wait_ge(t_scored, it * (2 * G * a["KT"]) + (a["t0"] + 2 * a["KT"] * (u + 1)))
                        load(a, it + 1, u)

                if a["kind"] == SELF:
                    max_to_q(0, 0)
                if a["k"] == 0:
                    context_parts(3)
                items(sp, step)

            for p in range(len(PHASES)):
                phase(p)
                if "att" in PHASES[p]:
                    attention(ATTS[PHASES[p]["att"]], p)
            last = len(PHASES) - 1
            for s in range(B):
                sp.wait_ge(mlp_added, nth("mlp", last, s))
                sp.dma_start(out[s].rearrange("(t p) c -> p t c", p=PT), X[:, s, :, :]).then_inc(stored, 16)
            sp.wait_ge(stored, 16 * B)

        @block.tensor
        def _(pe):
            pe.wait_ge(ld_vec, 16)
            pe.wait_ge(ld_id, 16)
            pe.transpose(bk[0][:, 0:N_VEC], VROW[0:N_VEC, :], IDF[0:N_VEC, 0:N_VEC]).then_inc(set_pe, 1)
            pe.wait_ge(ld_ada, 16)
            pe.wait_ge(set_dve, DVE["cond"])

            def modulation(first, chunks):
                for n in chunks:
                    raw = n < ADA_AT["L1_xcond_w_ada"]
                    mm = pe.matmul(bk[0 if first else 1][:, n * B:n * B + B], ADAW[:, n, :],
                                   COND[:, 0 if raw else 2, :], start=True, stop=True)
                mm.then_inc(set_pe, 1)

            modulation(True, range(2))

            def gate(n):
                pe.wait_ge(set_dve, DVE[f"diag{n}"])
                pe.matmul(bk[n % 2], ONES[:, :], DIAG[:, n % 2, :, :].rearrange("p a b -> p (a b)"),
                          start=True, stop=True).then_inc(set_pe, 1)

            def turn_masks():
                pe.wait_ge(set_dve, DVE["mask"])
                for kt in range(NT):
                    if kt >= 2:
                        pe.wait_ge(set_act, ACTS[f"mask{kt - 2}"])
                    for qt in range(NT):
                        mm = pe.transpose(bk[kt % 2].bitcast(bf16)[:, qt * PT:qt * PT + PT],
                                          MASKN[:, qt, kt * PT:kt * PT + PT], IDB[:, :])
                    mm.then_inc(set_pe, 1)

            def turn_context(src):
                for b in range(B):
                    mm = pe.transpose(bk[0][:, b * LC:b * LC + LC], src[:, b, :], IDF[0:LC, 0:LC])
                mm.then_inc(set_pe, 1)

            def context(l):
                kw, kc, vw, vc, kb, vb = CONTEXT[l]
                w_ready(pe, kw)
                src = CZT if l == 2 else CXT
                pe.wait_ge(set_act, ACTS["czt" if l == 2 else "cxt"])
                pe.matmul(bk[0][:, 0:B * LC], wt(kw, kc), src, start=True, stop=True).then_inc(set_pe, 1)
                for b in range(B):
                    o = bk[1][0:LC, b * C:b * C + C]
                    if vb:
                        pe.matmul(o, ONES[0:1, 0:LC], brow(vb, 1), start=True, stop=False)
                    mm = pe.matmul(o, src[:, b * LC:b * LC + LC], wt(vw, vc), start=not vb, stop=True)
                mm.then_inc(set_pe, 1)

            def free(dve_step, act_step):
                if dve_step:
                    pe.wait_ge(set_dve, DVE[dve_step])
                if act_step:
                    pe.wait_ge(set_act, ACTS[act_step])

            def extra(s):
                if s == 1:
                    pe.wait_ge(consts, CONSTS["ONES"])
                    modulation(False, range(2, N_ADA))
                elif s == 2:
                    pe.wait_ge(ld_ctx, 16)
                    free("scales", None)
                    turn_context(CTX)
                    context(0)
                    free("rest_0", "v_0")
                    gate(0)
                    gate(1)
                elif s == 3:
                    pe.wait_ge(ld_brow, 16)
                    free("rest_0", "gate1")
                    turn_masks()
                    free(None, "mask3")
                    gate(2)
                    gate(3)
                    free(None, "gate3")
                    context(1)
                elif s == 4:
                    free("rest_1", "v_1")
                    gate(4)
                    gate(5)
                    free("ctxn", "gate5")
                    turn_context(CTN)
                    context(2)
                elif s == 5:
                    free("rest_2", "v_2")
                    gate(6)
                    gate(7)
                    free(None, "gate7")
                    context(3)

            def entry(p):
                k = att_of(p)
                if k is not None:
                    att_over(pe, k, m_reduced)

            def turn_on(p, s):
                if s >= 1:
                    pe.wait_ge(ot_ready, nth("post", p, s - 1))
                pe.wait_ge(o_normed, ATTS[att_of(p)]["item0"] + G * (s + 1))
                for t in range(NT):
                    mm = pe.transpose(bk[0][:, t * PT:t * PT + PT], ON[:, s, t, :], IDF[:, :])
                mm.then_inc(on_turned, 1)

            def project_out(p, s):
                name, bias, _ = PHASES[p]["post"]
                w_ready(pe, name)
                pe.wait_ge(ot_ready, nth("post", p, s))
                if s >= 1:
                    pe.wait_ge(post_added, nth("post", p, s - 1))
                for t in range(NT):
                    o = bk[1][:, t * C:t * C + C]
                    if bias:
                        pe.matmul(o, ONES[0:1, 0:PT], brow(bias), start=True, stop=False)
                    mm = pe.matmul(o, OT_[:, s % 2, t * PT:t * PT + PT], wt(name), start=not bias, stop=True)
                mm.then_inc(out_done, 1)

            def turn_xn(p, s):
                pe.wait_ge(xn_ready, nth("ln", p, s))
                if s >= 1:
                    pe.wait_ge(h_ready, nth("ln", p, s - 1))
                elif att_of(p) is not None:
                    att_over(pe, att_of(p), exp_done)
                elif p:
                    pe.wait_ge(h_ready, nth("ln", p - 1, B - 1))
                for t in range(NT):
                    mm = pe.transpose(bk[2][:, t * PT:t * PT + PT], XN[:, s % 2, t, :], IDF[:, :])
                mm.then_inc(xn_turned, 1)

            def project(p, s):
                ph = PHASES[p]
                name, bias = ph["proj"]
                w_ready(pe, name)
                off = SHIFT if ph.get("roll") else 0
                h = HT[:, s % 2, off:off + L]
                pe.wait_ge(h_ready, nth("ln", p, s))
                if s >= 1:
                    pe.wait_ge(rest1[0], nth("q", p, s - 1))
                mm = pe.matmul(bk[3], wt(name, 0), h, start=True, stop=True)
                if ph.get("rope"):
                    pe.wait_ge(set_dve, DVE["rot"])
                    mm = pe.matmul(bk[4], WROT[:, 0, :], h, start=True, stop=True)
                mm.then_inc(proj_q, 1)
                if not ph.get("kv"):
                    return
                if s >= 1:
                    pe.wait_ge(rest1[1], nth("kv", p, s - 1))
                mm = pe.matmul(bk[5], wt(name, 1), h, start=True, stop=True)
                if ph.get("rope"):
                    mm = pe.matmul(bk[6], WROT[:, 1, :], h, start=True, stop=True)
                mm.then_inc(proj_k, 1)
                if s >= 1:
                    pe.wait_ge(v_ready, nth("kv", p, s - 1))
                elif p and att_of(p) is None:
                    pe.wait_ge(mlp_added, nth("mlp", p - 1, B - 1))
                elif p:
                    att_over(pe, att_of(p), o_normed)
                for t in range(NT):
                    o = bk[7][:, t * C:t * C + C]
                    if bias:
                        pe.matmul(o, ONES[0:1, 0:PT], brow(bias, 2), start=True, stop=False)
                    mm = pe.matmul(o, h[:, t * PT:t * PT + PT], wt(name, 2), start=not bias, stop=True)
                mm.then_inc(proj_v, 1)

            def up(p, s):
                w1, _, w2, b2, _, glu = PHASES[p]["mlp"]
                w_ready(pe, w2)
                pe.wait_ge(h_ready, nth("ln", p, s))
                h = HT[:, s % 2, 0:L]
                n = mlp_chunks(p)
                order = [c for j in range(NT) for c in ((j, NT + j) if glu else (j,))]
                for i, c in enumerate(order):
                    before = s * mlp_chunks(p) + i - 4
                    if before >= 0 and glu and before % 2:
                        pe.wait_ge(glu_done, before // 2 + 1)
                    elif before >= 0:
                        pe.wait_ge(act_done, ACT_FROM[p] + (before // 2 if glu else before) + 1)
                    pe.matmul(bk[3 + i % 4], wt(w1, c), h, start=True, stop=True).then_inc(up_done, 1)

            def down(p, s):
                w1, _, w2, b2, _, glu = PHASES[p]["mlp"]
                if s:
                    pe.wait_ge(mlp_added, nth("mlp", p, s - 1))
                else:
                    att_over(pe, att_of(p), o_normed)
                if glu:
                    pe.wait_ge(glu_done, NT * (s + 1))
                else:
                    pe.wait_ge(act_done, ACT_FROM[p] + NT * (s + 1))
                for t in range(NT):
                    o = bk[7][:, t * C:t * C + C]
                    pe.matmul(o, ONES[0:1, 0:PT], brow(b2), start=True, stop=False)
                    for c in range(NT):
                        mm = pe.matmul(o, UT[:, s % 2, c, t * PT:t * PT + PT], wt(w2, c),
                                       start=False, stop=(c == NT - 1))
                mm.then_inc(down_done, 1)

            def phase(p):
                is_mlp = "mlp" in PHASES[p]
                for s in range(B + 2):
                    joins = "post" in PHASES[p] and joined(p) <= s < B
                    if joins:
                        turn_on(p, s)
                    if s >= 2:
                        (up if is_mlp else project)(p, s - 2)
                    if joins:
                        project_out(p, s)
                    if 1 <= s <= B:
                        turn_xn(p, s - 1)
                    if s >= 2 and is_mlp:
                        down(p, s - 2)
                    if p == 0:
                        extra(s)

            def attention(a, p):
                KT, KP, CM, LA, kind = a["KT"], a["KP"], a["CM"], a["LA"], a["kind"]
                if p == 0:
                    pe.wait_ge(set_dve, DVE["rest_3"])
                    pe.wait_ge(set_act, ACTS["v_3"])
                masked, topk = a.get("mask"), a.get("topk")
                pe.wait_ge(rest1[0], nth("q", p, B - 1))
                pe.wait_ge(h_ready, nth("ln", p, B - 1))
                if PHASES[p].get("kv"):
                    pe.wait_ge(rest1[1], nth("kv", p, B - 1))
                    pe.wait_ge(v_ready, nth("kv", p, B - 1))
                if "post" in PHASES[p]:
                    pe.wait_ge(post_added, nth("post", p, B - 1))
                if a["rows_set"]:
                    pe.wait_ge(rows_set, a["rows_set"])

                def m_scores(it, u, c):
                    it, u = (it, u) if u < G else (it + 1, u - G)
                    if c == 0:
                        pe.wait_ge(loaded[u], it * a["ldn"] + a["ld0"])
                    if topk:
                        pe.wait_ge(top_read, it * (G * CM) + (BIAS + CM * u + c - 1))
                    else:
                        pe.wait_ge(m_reduced, it * (G * CM) + (a["m0"] + CM * u + c - 1))
                    o = bank[c % 2]
                    if kind == SELF:
                        h, qt = c // NT, c % NT
                        mm = pe.matmul(o[:, :], QS[0:MAX0, u, h, qt * PT:qt * PT + PT], KS[0:MAX0, u, h, :],
                                       start=True, stop=True)
                    elif kind == WINDOW:
                        for t in range(NT):
                            w = slice(t * PT, t * PT + PT)
                            mm = pe.matmul(o[:, w], QS[:, u, c, w], KS[:, u, c, w], start=True, stop=True)
                    else:
                        for h in range(G):
                            oo = o[:, h * PT:h * PT + LC]
                            mm = pe.matmul(oo, QS[:, u, h, c * PT:c * PT + PT], KS[:, u, h, 0:LC],
                                           start=True, stop=True)
                    mm.then_inc(m_scored, 1)

                def turn_max(it, u):
                    it, u = (it, u) if u < G else (it + 1, u - G)
                    pe.wait_ge(max_split, it * G + (a["item0"] + u + 1))
                    for qt in range(NT):
                        mm = pe.transpose(b7[:, :].bitcast(bf16)[0:3 * G, qt * PT:qt * PT + PT],
                                          MP[:, u, qt, :, :].rearrange("p h s -> p (h s)"), IDB[:, :])
                    mm.then_inc(max_turned, 1)

                def t_scores(it, u, kt, pr):
                    it, u = (it, u) if u < G else (it + 1, u - G)
                    if kt == 0 and pr == 0:
                        if kind == SELF:
                            pe.wait_ge(max_rows[u], it * 16 + 16 * (B * a["selfs"] + 1))
                        else:
                            pe.wait_ge(max_copied, it * G + (a["item0"] + u + 1))
                    pe.wait_ge(exp_done, it * (2 * G * KT) + (a["t0"] + 2 * (KT * u + kt) + pr - 1))
                    for x in range(2):
                        h = 2 * pr + x
                        o = ST[pr][0:KP, x, :]
                        if kind == SELF:
                            mm = pe.matmul(o, KS[:, u, h, kt * PT:kt * PT + PT], QS[:, u, h, :],
                                           start=True, stop=not masked)
                            if masked:
                                mm = pe.matmul(o, IDB[:, :], MASKT[:, kt, :], start=False, stop=True)
                            continue
                        pe.matmul(o, SELM[:, h, 0:KP], MTS[:, u, :], start=True, stop=False)
                        if kind == WINDOW:
                            for t in range(NT):
                                w = slice(t * PT, t * PT + PT)
                                mm = pe.matmul(o[:, w], KS[:, u, h, w], QS[:, u, h, w],
                                               start=False, stop=(t == NT - 1))
                            continue
                        mm = pe.matmul(o, KS[:, u, h, 0:LC], QS[:, u, h, :], start=False, stop=not topk)
                        if topk:
                            for qt in range(NT):
                                mm = pe.matmul(o[:, qt * PT:qt * PT + PT], REST[:, u, qt, h, :], IDNEG[:, :],
                                               start=False, stop=(qt == NT - 1))
                    mm.then_inc(t_scored, 1)

                def pv(it, u, kt):
                    n = KT * u + kt
                    pe.wait_ge(exp_done, it * (2 * G * KT) + (a["t0"] + 2 * n + 2))
                    if kt == 0:
                        pe.wait_ge(ot_copied, it * G + (a["item0"] + u))
                        pe.wait_ge(vg_ready, it * G + (a["item0"] + u + 1))
                    for t in range(NT if kind == WINDOW else 1):
                        w = slice(t * PT, t * PT + PT) if kind == WINDOW else slice(0, L)
                        for h in range(G):
                            mm = pe.matmul(b6[32 * h:32 * h + 32, w],
                                           VG[:, u, t if kind == WINDOW else kt, h, :],
                                           P[:, n % 2, h, w], start=(kt == 0), stop=(kt == KT - 1),
                                           tile_position=(0, 32 * h))
                    mm.then_inc(pv_done, 1)

                def turn_out(it, u, prior):
                    back = 1 if prior else 0
                    pe.wait_ge(ot_copied, it * G + (a["item0"] + u + 1 - back))
                    for qt in range(NT):
                        mm = pe.transpose(b7[:, qt * PT:qt * PT + PT], OTS[:, (u - back) % 2, qt * PT:qt * PT + PT],
                                          IDF[:, :])
                    mm.then_inc(o_turned, 1)

                def b7_free(it, u, maxes, outs):
                    pe.wait_ge(max_copied, it * G + (a["item0"] + u + maxes))
                    pe.wait_ge(o_normed, it * G + (a["item0"] + u + outs))

                def item(it, u, last, first=False):
                    left = G - u if last else 2 * G
                    per = CM // KT
                    for kt in range(KT):
                        def m(c):
                            if first and kind == SELF:
                                for n in (2 * (kt * per + c), 2 * (kt * per + c) + 1):
                                    m_scores(it, 1 + n // CM, n % CM)
                            elif left > LA:
                                m_scores(it, u + LA, kt * per + c)

                        def t(pr):
                            if kt + 1 < KT:
                                t_scores(it, u, kt + 1, pr)
                            elif left > 1:
                                t_scores(it, u + 1, 0, pr)

                        ending = last and u == G - 1
                        m(0)
                        t(0)
                        m(1)
                        t(1)
                        m(2)
                        if ending and KT == 1:
                            entry(p + 1)
                            turn_on(p + 1, 0)
                        if kt == (2 if first and kind == SELF else 0) and left > LA - 1:
                            b7_free(it, u, LA - 1, -1)
                            turn_max(it, u + LA - 1)
                        if kind == SELF and not masked:
                            m(3)
                            pv(it, u, kt)
                        else:
                            pv(it, u, kt)
                            m(3)
                        if kt == 0 and not first:
                            b7_free(it, u, LA if left > LA - 1 else left, -1)
                            turn_out(it, u, True)
                        if ending and KT == 1:
                            project_out(p + 1, 0)
                        elif ending and kt == 0:
                            entry(p + 1)
                            turn_on(p + 1, 0)
                        elif ending and kt == 1:
                            project_out(p + 1, 0)
                            turn_on(p + 1, 1)
                        elif ending and kt == 2:
                            project_out(p + 1, 1)

                for u in range(1 if kind == SELF else LA):
                    for c in range(CM):
                        m_scores(0, u, c)
                for u in range(LA - 1):
                    if u:
                        b7_free(0, 0, u, 0)
                    turn_max(0, u)
                for pr in range(2):
                    t_scores(0, 0, 0, pr)
                with_first(pe, a, item)
                b7_free(B - 1, G, 0, -1)
                turn_out(B - 1, G, True)

            def with_first(eng, a, item):
                for u in range(G):
                    item(0, u, False, first=(u == 0))
                with eng.Fori(1, B - 1) as it:
                    for u in range(G):
                        item(it, u, False)
                for u in range(G):
                    item(B - 1, u, True)

            for p in range(len(PHASES)):
                phase(p)
                if "att" in PHASES[p]:
                    attention(ATTS[PHASES[p]["att"]], p)

        @block.scalar
        def _(act):
            ACT_ID, ACT_EXP = ACT.Identity, ACT.Exp
            for s in (exp_done, ot_copied, max_copied):
                act.sem_inc(s, BIAS)
            act.preload_act_table(ACT_EXP)
            act.wait_ge(set_pe, 1)
            act.activation(COL[:, :], bk[0][:, 0:N_VEC], ACT.Copy).then_inc(set_act, 1)
            act.wait_ge(set_act, 1)
            act.activation(COND[:, 1, :], COL[:, VEC_AT["cond_1024"]:VEC_AT["cond_1024"] + B], ACT_EXP,
                           scale=-1.0).then_inc(set_act, 1)

            def part1_and_v(l):
                _, _, _, _, kb, vb = CONTEXT[l]
                if l >= 2:
                    act.wait_ge(ctx_k_dma[l - 2], 16 * 3)
                act.wait_ge(set_pe, PES[f"k_{l}"])
                act.activation(CPARTS[l % 2][:, 0], bk[0][:, 0:B * LC], ACT_ID if kb else ACT.Copy,
                               **({"bias": col(kb)} if kb else {})).then_inc(set_act, 1)
                act.wait_ge(set_pe, PES[f"v_{l}"])
                act.wait_ge(consts, CONSTS["VC"])
                act.activation(VC[:, l, :, :, 0:D].rearrange("p b h d -> p (b h) d"),
                               bk[1][0:LC, :].rearrange("p (h d) -> p h d", d=D), ACT.Copy).then_inc(set_act, 1)

            def part2_of(l):
                act.wait_ge(set_dve, DVE[f"rest_{l}"])
                act.activation(CPARTS[l % 2][:, 1], CREST, ACT.Copy).then_inc(set_act, 1)

            def gate(n):
                act.wait_ge(set_pe, PES[f"gate{n}"])
                act.activation(GATE[:, n, :, :], bk[n % 2].rearrange("p (b c) -> p b c", b=B), ACT.Copy
                               ).then_inc(set_act, 1)

            def extra(s):
                if s == 2:
                    act.wait_ge(set_pe, PES["cxt"])
                    act.activation(CXT, bk[0][:, 0:B * LC], ACT.Copy).then_inc(set_act, 1)
                    part1_and_v(0)
                    gate(0)
                    gate(1)
                elif s == 3:
                    part2_of(0)
                    for kt in range(NT):
                        act.wait_ge(set_pe, PES[f"mask{kt}"])
                        act.activation(MASKT[:, kt, :], bk[kt % 2].bitcast(bf16)[:, 0:L], ACT.Copy
                                       ).then_inc(set_act, 1)
                    gate(2)
                    gate(3)
                    part1_and_v(1)
                elif s == 4:
                    part2_of(1)
                    gate(4)
                    gate(5)
                    act.wait_ge(set_pe, PES["czt"])
                    act.wait_ge(set_dve, DVE["scales"])
                    for b in range(B):
                        i = act.activation(CZT[:, b * LC:b * LC + LC], bk[0][:, b * LC:b * LC + LC], ACT_ID,
                                           scale=SCSH[:, 0, LN_KV, b:b + 1], bias=SCSH[:, 1, LN_KV, b:b + 1])
                    i.then_inc(set_act, 1)
                    part1_and_v(2)
                elif s == 5:
                    part2_of(2)
                    gate(6)
                    gate(7)
                    part1_and_v(3)
                    part2_of(3)

            def post(p, s):
                act.wait_ge(on_turned, nth("post", p, s))
                if s >= 2:
                    act.wait_ge(out_done, nth("post", p, s - 2))
                if PHASES[p - 1].get("roll"):
                    act.activation(OT_[:, s % 2, SHIFT:L], bk[0][:, 0:L - SHIFT], ACT.Copy)
                    act.activation(OT_[:, s % 2, 0:SHIFT], bk[0][:, L - SHIFT:L], ACT.Copy).then_inc(ot_ready, 1)
                else:
                    act.activation(OT_[:, s % 2, :], bk[0], ACT.Copy).then_inc(ot_ready, 1)

            def scaled(p, s):
                ln = PHASES[p]["ln"]
                sc, sh = SCSH[:, 0, ln, s:s + 1], SCSH[:, 1, ln, s:s + 1]
                act.wait_ge(xn_turned, nth("ln", p, s))
                if p == 0:
                    act.wait_ge(set_dve, DVE["scale0"])
                if p or s >= 2:
                    h_last_read(act, *((p, s - 2) if s >= 2 else (p - 1, s + 2)))
                if PHASES[p].get("roll"):
                    act.activation(HT[:, s % 2, L:L + SHIFT], bk[2][:, 0:SHIFT], ACT_ID, scale=sc, bias=sh)
                act.activation(HT[:, s % 2, 0:L], bk[2], ACT_ID, scale=sc, bias=sh).then_inc(h_ready, 1)

            def first_parts(p, s):
                ph = PHASES[p]
                bias = ph["proj"][1]
                before = prior_write(p, s)
                if p == 0 and s == 0:
                    act.wait_ge(consts, CONSTS["V"])
                if before:
                    act.wait_ge(scratch_written[before[0]], before[1])
                for side in range(2 if ph.get("kv") else 1):
                    step = "kv" if side else "q"
                    if ph.get("rope"):
                        act.wait_ge(q_roped, 2 * s + side + 1)
                        src = RA[:, side, :]
                    else:
                        act.wait_ge((proj_q, proj_k)[side], nth(step, p, s))
                        src = bk[5 if side else 3]
                    act.activation(PARTS[:, s % 2, side, 0, :], src, ACT_ID if bias else ACT.Copy,
                                   **({"bias": col(bias, side)} if bias else {})).then_inc(part1[side], 1)
                if ph.get("kv"):
                    act.wait_ge(proj_v, nth("kv", p, s))
                    act.activation(V[:, s, :, :, 0:D].rearrange("p t h d -> p (t h) d"),
                                   bk[7].rearrange("p (h d) -> p h d", d=D), ACT.Copy).then_inc(v_ready, 1)
                for side in range(2 if ph.get("kv") else 1):
                    act.wait_ge(rest1[side], nth("kv" if side else "q", p, s))
                    act.activation(PARTS[:, s % 2, side, 1, :], RA[:, side, :], ACT.Copy).then_inc(part2[side], 1)

            def mlp(p, s):
                w1, b1, _, _, _, glu = PHASES[p]["mlp"]
                for j in range(NT):
                    act.wait_ge(up_done, nth_chunk(p, s, 2 * j if glu else j))
                    if s >= 2:
                        act.wait_ge(down_done, nth("mlp", p, s - 2))
                    i = 2 * j if glu else j
                    act.activation(UT[:, s % 2, j, :], bk[3 + i % 4], ACT.Silu if glu else ACT.Gelu_apprx_tanh,
                                   bias=col(b1, j)).then_inc(act_done, 1)

            def phase(p):
                for s in range(B + 2):
                    if "post" in PHASES[p] and joined(p) <= s < B:
                        post(p, s)
                    if s >= 2:
                        (mlp if "mlp" in PHASES[p] else first_parts)(p, s - 2)
                    if 1 <= s <= B:
                        scaled(p, s - 1)
                    if p == 0:
                        extra(s)

            def attention(a, p):
                KT, KP, LA, kind = a["KT"], a["KP"], a["LA"], a["kind"]
                act.preload_act_table(ACT_EXP)

                def exps(it, u, kt):
                    n = KT * u + kt
                    for pr in range(2):
                        act.wait_ge(t_scored, it * (2 * G * KT) + (a["t0"] + 2 * n + pr + 1))
                        act.wait_ge(pv_done, it * (G * KT) + (a["u0"] + n - 1))
                        act.activation(P[0:KP, n % 2, 2 * pr:2 * pr + 2, :], ST[pr][0:KP, :, :], ACT_EXP, scale=SCALE
                                       ).then_inc(exp_done, 1)

                def copy_max(it, u):
                    it, u = (it, u) if u < G else (it + 1, u - G)
                    act.wait_ge(max_turned, it * G + (a["item0"] + u + 1))
                    act.wait_ge(t_scored, it * (2 * G * KT) + (a["t0"] + 2 * KT * (u - 3)))
                    act.activation(MTS[0:MAXES, u, :], b7[:, :].bitcast(bf16)[0:3 * G, 0:L], ACT.Copy
                                   ).then_inc(max_copied, 1)

                def copy_out(it, u):
                    act.wait_ge(pv_done, it * (G * KT) + (a["u0"] + KT * (u + 1)))
                    act.wait_ge(o_turned, it * G + (a["item0"] + u - 1))
                    act.activation(OTS[:, u % 2, :], b6[:, :], ACT.Copy).then_inc(ot_copied, 1)

                def item(it, u, last, first=False):
                    left = G - u if last else 2 * G
                    for kt in range(KT):
                        exps(it, u, kt)
                        if kt == 0 and not first:
                            copy_out(it, u - 1)
                        if kt == (2 if first and kind == SELF else 0) and left > LA - 1:
                            copy_max(it, u + LA - 1)
                        if last and u == G - 1 and kt < joined(p + 1):
                            post(p + 1, kt)

                for u in range(LA - 1):
                    copy_max(0, u)
                for u in range(G):
                    item(0, u, False, first=(u == 0))
                with act.Fori(1, B - 1) as it:
                    for u in range(G):
                        item(it, u, False)
                for u in range(G):
                    item(B - 1, u, True)
                copy_out(B - 1, G - 1)

            for p in range(len(PHASES)):
                phase(p)
                if "att" in PHASES[p]:
                    attention(ATTS[PHASES[p]["att"]], p)

        @block.vector
        def _(dve):
            steps = [0]

            def link(i):
                steps[0] += 1
                i.then_inc(dve_step, 1)
                dve.wait_ge(dve_step, steps[0])

            for s in (m_reduced, o_inverted, o_normed, top_found, top_read):
                dve.sem_inc(s, BIAS)
            cond = COL[:, VEC_AT["cond_1024"]:VEC_AT["cond_1024"] + B]
            dve.wait_ge(ld_id, 16)
            dve.tensor_copy(IDB[:, :], IDF[:, :])
            dve.tensor_scalar(IDNEG[:, :], IDF[:, :], NEG, None, ALU.mult)

            dve.wait_ge(set_act, 2)
            dve.tensor_copy(COND[:, 0, :], cond)
            link(dve.tensor_scalar(COND[:, 1, :], COND[:, 1, :], 1.0, None, ALU.add))
            link(dve.reciprocal(COND[:, 1, :], COND[:, 1, :]))
            dve.tensor_tensor(COND[:, 2, :], cond, COND[:, 1, :], ALU.mult).then_inc(set_dve, 1)
            mod0, mod = (bk[i][:, 0:128].rearrange("p (n b) -> p n b", b=B) for i in range(2))

            def put(kind, ln, ada_name, chunk, bias_name, plus=0.0):
                src = mod0 if ada_name == "L0_xcond_adaLN_W" and chunk < 2 else mod
                return dve.tensor_scalar(SCSH[:, kind, ln, :], src[:, ADA_AT[ada_name] + chunk, :],
                                         col(bias_name, chunk), plus, ALU.add, ALU.add)

            def layer0_scale(j, w):
                put(1, j, "L0_xcond_adaLN_W", 3 * j, "L0_xcond_adaLN_b")
                link(put(0, j, "L0_xcond_adaLN_W", 3 * j + 1, "L0_xcond_adaLN_b", 1.0))
                return dve.tensor_scalar(SCSH[:, 0, j, :], SCSH[:, 0, j, :], col(w), None, ALU.mult)

            def scales():
                dve.wait_ge(set_pe, PES["mod"])
                for n, (bias_name, chunk) in enumerate(GATES):
                    ada_name = {"L0_xcond_adaLN_b": "L0_xcond_adaLN_W", "L1_xcond_b_ada": "L1_xcond_w_ada",
                                "L3_xcond_ada_b": "L3_xcond_ada_w"}[bias_name]
                    dve.tensor_scalar(GCOL[:, n, :], mod[:, ADA_AT[ada_name] + chunk, :], col(bias_name, chunk),
                                      None, ALU.add)
                for j, w in enumerate(("L0_xcond_normc_w", "L0_xcond_norm2_w")):
                    layer0_scale(1 + j, w)
                for j in range(3):
                    put(1, 3 + j, "L1_xcond_w_ada", 3 * j, "L1_xcond_b_ada")
                    put(0, 3 + j, "L1_xcond_w_ada", 3 * j + 1, "L1_xcond_b_ada", 1.0)
                for ln, ada_name, bias_name in ((6, "L2_xcond_Wss_q", "L2_xcond_bss_q"),
                                                (LN_KV, "L2_xcond_Wss_kv", "L2_xcond_bss_kv")):
                    put(0, ln, ada_name, 0, bias_name, 1.0)
                    put(1, ln, ada_name, 1, bias_name)
                for ln, chunk in ((7, 0), (9, 3)):
                    put(1, ln, "L3_xcond_ada_w", chunk, "L3_xcond_ada_b")
                    put(0, ln, "L3_xcond_ada_w", chunk + 1, "L3_xcond_ada_b", 1.0)
                dve.tensor_copy(SCSH[:, 0, 8, :], col("L3_xcond_norm2_g").broadcast_to([C, B]))
                dve.tensor_copy(SCSH[:, 1, 8, :], col("L3_xcond_norm2_b").broadcast_to([C, B])
                                ).then_inc(set_dve, 1)
                dve.wait_ge(set_dve, DVE["scales"])

            def diag(n):
                if n >= 2:
                    dve.wait_ge(set_pe, PES[f"gate{n - 2}"])
                dve.tensor_tensor(DIAG[:, n % 2, :, :], IDF[:, None, :].broadcast_to([C, B, C]),
                                  GCOL[:, n, :][:, :, None].broadcast_to([C, B, C]), ALU.mult
                                  ).then_inc(set_dve, 1)

            def rotated_weights():
                dve.wait_ge(ld_w0, 16)
                for i in range(2):
                    w = wt("L0_xcond_qkv_W", i).rearrange("p (h d) -> p h d", d=D)
                    r = WROT[:, i, :].rearrange("p (h d) -> p h d", d=D)
                    dve.tensor_scalar(r[:, :, 0:D // 2], w[:, :, D // 2:D], -1.0, None, ALU.mult)
                    last = dve.tensor_copy(r[:, :, D // 2:D], w[:, :, 0:D // 2])
                last.then_inc(set_dve, 1)

            def masks():
                dve.wait_ge(ld_side, 16)
                dve.tensor_copy(SIDE[:, :], SIDE32)
                dve.wait_ge(ld_mask, 32)
                dve.tensor_scalar(MROW[:, :, :].rearrange("p b k -> p (b k)"), MKU, -NEG, NEG, ALU.mult,
                                  ALU.add)
                dve.tensor_scalar(MASKN, MSKU, -NEG, NEG, ALU.mult, ALU.add).then_inc(set_dve, 1)

            def normalise_context():
                dve.wait_ge(ld_ctx, 16)
                for b in range(B):
                    i = dve.bn_stats(STAT[0:LC, b, :], CTX[:, b, :])
                link(i)
                for b in range(B):
                    i = dve.bn_aggr(MV[0:LC, b, :], STAT[0:LC, b, :])
                i.then_inc(set_dve, 1)
                dve.wait_ge(set_dve, DVE["cstat"])
                dve.wait_ge(set_pool, 1)
                for b in range(B):
                    i = dve.tensor_scalar(CTN[:, b, :], CTX[:, b, :], MV[0:LC, b, 0:1], RSTD[0:LC, 2, b:b + 1],
                                          ALU.subtract, ALU.mult)
                i.then_inc(set_dve, 1)
                dve.wait_ge(set_dve, DVE["ctxn"])

            def rest_of(l):
                kb = CONTEXT[l][4]
                dve.wait_ge(set_act, ACTS[f"part1_{l}"])
                if kb:
                    i = dve.scalar_tensor_tensor(out=CREST, in0=bk[0][:, 0:B * LC], scalar=col(kb),
                                                 in1=CPARTS[l % 2][:, 0], op0=ALU.add, op1=ALU.subtract)
                else:
                    i = dve.tensor_tensor(CREST, bk[0][:, 0:B * LC], CPARTS[l % 2][:, 0], ALU.subtract)
                i.then_inc(set_dve, 1)

            def part3_of(l):
                dve.wait_ge(set_act, ACTS[f"part2_{l}"])
                dve.wait_ge(set_dve, DVE[f"rest_{l}"])
                dve.tensor_tensor(CPARTS[l % 2][:, 2], CREST, CPARTS[l % 2][:, 1], ALU.subtract
                                  ).then_inc(set_dve, 1)
                dve.wait_ge(set_dve, DVE[f"part3_{l}"])

            def extra(s):
                if s == 0:
                    dve.wait_ge(set_pe, PES["mod0"])
                    layer0_scale(0, "L0_xcond_norm1_w").then_inc(set_dve, 1)
                    rotated_weights()
                elif s == 1:
                    masks()
                    dve.memset(VG[:, :, :, :, :], 0.0)
                    scales()
                elif s == 2:
                    diag(0)
                    diag(1)
                    rest_of(0)
                    diag(2)
                    diag(3)
                elif s == 3:
                    part3_of(0)
                    rest_of(1)
                    normalise_context()
                    diag(4)
                    diag(5)
                elif s == 4:
                    part3_of(1)
                    rest_of(2)
                    diag(6)
                    diag(7)
                elif s == 5:
                    part3_of(2)
                    rest_of(3)
                    part3_of(3)

            def post(p, s):
                gate = PHASES[p]["post"][2]
                dve.wait_ge(out_done, nth("post", p, s))
                ps = bk[1].rearrange("p (t c) -> p t c", t=NT)
                if gate is None:
                    dve.tensor_tensor(X[:, s, :, :], ps, X[:, s, :, :], ALU.add).then_inc(post_added, 1)
                else:
                    link(dve.tensor_tensor(TMP[:, :, :], ps,
                                           GATE[:, gate, s, :][:, None, :].broadcast_to([PT, NT, C]), ALU.mult))
                    dve.tensor_tensor(X[:, s, :, :], TMP[:, :, :], X[:, s, :, :], ALU.add).then_inc(post_added, 1)
                dve.wait_ge(post_added, nth("post", p, s))

            def stats(p, s):
                if p == 0:
                    dve.wait_ge(ld_x[s], 16)
                if p or s:
                    dve.wait_ge(xn_ready, nth("ln", p, s) - 1)
                    dve.wait_ge(rstd_ready, nth("ln", p, s) - 1)
                for t in range(NT):
                    i = dve.bn_stats(STAT[:, t, :], X[:, s, t, :])
                link(i)
                for t in range(NT):
                    i = dve.bn_aggr(MV[:, t, :], STAT[:, t, :])
                i.then_inc(stats_ready, 1)

            def normalise(p, s):
                dve.wait_ge(rstd_ready, nth("ln", p, s))
                if p or s >= 2:
                    dve.wait_ge(xn_turned, nth("ln", p, s) - 2)
                dve.wait_ge(stats_ready, nth("ln", p, s))
                for t in range(NT):
                    i = dve.tensor_scalar(XN[:, s % 2, t, :], X[:, s, t, :], MV[:, t, 0:1], RSTD[:, s % 2, t:t + 1],
                                          ALU.subtract, ALU.mult)
                i.then_inc(xn_ready, 1)

            def join(p, s):
                if "post" in PHASES[p]:
                    post(p, s)
                stats(p, s)
                normalise(p, s)

            def rests(p, s):
                ph = PHASES[p]
                bias = ph["proj"][1]
                sides = range(2 if ph.get("kv") else 1)
                if ph.get("rope"):
                    dve.wait_ge(ld_rope, 16)
                    for side in sides:
                        dve.wait_ge((proj_q, proj_k)[side], s + 1)
                        if s:
                            dve.wait_ge(part3[side], s)
                        dve.tensor_tensor(RA[:, side, :], bk[5 if side else 3], COS, ALU.mult)
                        link(dve.tensor_tensor(TMP[:, :, :].rearrange("p a b -> p (a b)"), bk[6 if side else 4], SIN,
                                               ALU.mult))
                        dve.tensor_tensor(RA[:, side, :], RA[:, side, :], TMP[:, :, :].rearrange("p a b -> p (a b)"),
                                          ALU.add).then_inc(q_roped, 1)
                        dve.wait_ge(q_roped, 2 * s + side + 1)
                for side in sides:
                    n = nth("kv" if side else "q", p, s)
                    src = RA[:, side, :] if ph.get("rope") else bk[5 if side else 3]
                    dve.wait_ge(part1[side], n)
                    if n >= 2:
                        dve.wait_ge(part3[side], n - 1)
                    if bias:
                        i = dve.scalar_tensor_tensor(out=RA[:, side, :], in0=src, scalar=col(bias, side),
                                                     in1=PARTS[:, s % 2, side, 0, :], op0=ALU.add, op1=ALU.subtract)
                    else:
                        i = dve.tensor_tensor(RA[:, side, :], src, PARTS[:, s % 2, side, 0, :], ALU.subtract)
                    i.then_inc(rest1[side], 1)
                for side in sides:
                    dve.wait_ge(part2[side], nth("kv" if side else "q", p, s))
                    dve.tensor_tensor(PARTS[:, s % 2, side, 2, :], RA[:, side, :], PARTS[:, s % 2, side, 1, :],
                                      ALU.subtract).then_inc(part3[side], 1)

            def glu(p, s):
                w1, b1, _, _, gate, glu = PHASES[p]["mlp"]
                if glu:
                    for j in range(NT):
                        dve.wait_ge(act_done, ACT_FROM[p] + NT * s + j + 1)
                        dve.wait_ge(up_done, nth_chunk(p, s, 2 * j + 1))
                        dve.scalar_tensor_tensor(out=UT[:, s % 2, j, :], in0=bk[3 + (2 * j + 1) % 4],
                                                 scalar=col(b1, NT + j), in1=UT[:, s % 2, j, :], op0=ALU.add,
                                                 op1=ALU.mult).then_inc(glu_done, 1)

            def mlp_add(p, s):
                gate = PHASES[p]["mlp"][4]
                dve.wait_ge(down_done, nth("mlp", p, s))
                ps = bk[7].rearrange("p (t c) -> p t c", t=NT)
                link(dve.tensor_tensor(TMP[:, :, :], ps, GATE[:, gate, s, :][:, None, :].broadcast_to([PT, NT, C]),
                                       ALU.mult))
                dve.tensor_tensor(X[:, s, :, :], TMP[:, :, :], X[:, s, :, :], ALU.add).then_inc(mlp_added, 1)
                dve.wait_ge(mlp_added, nth("mlp", p, s))

            def phase(p):
                is_mlp = "mlp" in PHASES[p]
                for s in range(B + 2):
                    if s >= 2:
                        (glu if is_mlp else rests)(p, s - 2)
                    if joined(p) <= s < B:
                        join(p, s)
                    if s >= 2 and is_mlp:
                        mlp_add(p, s - 2)
                    if p == 0:
                        extra(s)

            def attention(a, p):
                KT, CM, kind = a["KT"], a["CM"], a["kind"]

                def reduce(it, u, c, first=False):
                    it, u = (it, u) if u < G else (it + 1, u - G)
                    if c == 0:
                        dve.wait_ge(max_split, it * G + (a["item0"] + u - 3))
                    if a.get("topk"):
                        top16(it, u, c, first)
                        return
                    dve.wait_ge(m_scored, it * (G * CM) + (a["m0"] + CM * u + c + 1))
                    ps = bank[c % 2]
                    if kind == SELF:
                        h, qt = c // NT, c % NT
                        o = V8[:, u, qt, h, 0:1]
                        if a.get("mask"):
                            dve.wait_ge(m_reduced, it * (G * CM) + (a["m0"] + CM * u + c - 1))
                            dve.sem_inc(dve_gate, 1)
                            i = dve.tensor_tensor_reduce(JUNK[:, c % 2, :], ps[:, :], MASKN[:, qt, :], 1.0, LOW,
                                                         ALU.add, ALU.max, o)
                        else:
                            i = dve.tensor_reduce(o, ps[:, :], AX.X, ALU.max)
                    elif kind == WINDOW:
                        i = dve.tensor_reduce(V8[:, u, :, c, 0], ps[:, :].rearrange("p (t k) -> p t k", t=NT), AX.X,
                                              ALU.max)
                    else:
                        i = dve.tensor_reduce(V8[:, u, c, :, 0], ps[:, :].rearrange("p (h k) -> p h k", h=G)[:, :, 0:LC],
                                              AX.X, ALU.max)
                    i.then_inc(m_reduced, 1)

                def top16(it, u, c, first):
                    ps = bank[c % 2][:, :].rearrange("p (h k) -> p h k", h=G)
                    dve.wait_ge(m_scored, it * (G * CM) + (a["m0"] + CM * u + c + 1))
                    dve.sem_inc(dve_gate, 1)
                    dve.wait_ge(rest_marked, it * (G * CM) + (BIAS + CM * u + c - 3))
                    dve.sem_inc(dve_gate, 1)
                    for h in range(G):
                        i = dve.max(V8[:, u, c, h, :], ps[:, h, 0:LC])
                    i.then_inc(top_found, 1)
                    n = CM * u + c
                    if not first:
                        dve.wait_ge(top_read, it * (G * CM) + (BIAS + n))
                        dve.sem_inc(dve_gate, 1)
                        for h in range(G):
                            i = dve.max(V8B[:, (c - 1) % 2, h, :], TK[:, (c - 1) % NT, h, :])
                        i.then_inc(top_found, 1)
                    dve.wait_ge(top_found, it * (2 * G * CM) + (BIAS + 2 * n + 1))
                    dve.sem_inc(dve_gate, 1)
                    for h in range(G):
                        i = dve.match_replace(TK[:, c, h, :], V8[:, u, c, h, :], ps[:, h, 0:LC], LOW)
                    i.then_inc(top_read, 1)
                    if first:
                        dve.sem_inc(top_found, 1)
                    else:
                        dve.wait_ge(top_found, it * (2 * G * CM) + (BIAS + 2 * n + 2))
                        dve.sem_inc(dve_gate, 1)
                        for h in range(G):
                            i = dve.match_replace(TK[:, (c - 1) % NT, h, :], V8B[:, (c - 1) % 2, h, :],
                                                  TK[:, (c - 1) % NT, h, :], LOW)
                        i.then_inc(m_reduced, 1)

                def top16_end():
                    dve.drain()
                    for h in range(G):
                        dve.max(V8B[:, (NT - 1) % 2, h, :], TK[:, NT - 1, h, :])
                    dve.drain()
                    for h in range(G):
                        i = dve.match_replace(TK[:, NT - 1, h, :], V8B[:, (NT - 1) % 2, h, :], TK[:, NT - 1, h, :], LOW)
                    i.then_inc(m_reduced, 1)

                def norm(it, u):
                    dve.wait_ge(o_turned, it * G + (a["item0"] + u + 1))
                    ps = b7[:, :].rearrange("p (t h d) -> p t h d", t=NT, h=G)
                    dve.reciprocal(RC[:, u % 2, :, :], ps[:, :, :, D]).then_inc(o_inverted, 1)
                    dve.wait_ge(o_inverted, it * G + (a["item0"] + u + 1))
                    b, g = (it, u) if u >= 0 else (it - 1, G - 1)
                    o = ON[:, bass.ds(b, 1), :, g * G * D:(g + 1) * G * D].rearrange(
                        "p o t (h d) -> p (o t) h d", d=D)
                    dve.tensor_tensor(o, ps[:, :, :, 0:D],
                                      RC[:, u % 2, :, :][:, :, :, None].broadcast_to([PT, NT, G, D]), ALU.mult
                                      ).then_inc(o_normed, 1)

                def item(it, u, last, first=False):
                    left = G - u if last else 2 * G
                    for kt in range(KT):
                        if left > a["LA"]:
                            for c in range(kt * CM // KT, (kt + 1) * CM // KT):
                                reduce(it, u + a["LA"], c)
                            if a.get("topk") and last:
                                top16_end()
                        if kt == 0 and not first:
                            norm(it, u - 1)

                if p == 0:
                    dve.wait_ge(ctx_k_dma[2], 16 * 3)
                for u in range(a["LA"]):
                    for c in range(CM):
                        reduce(0, u, c, first=(u == c == 0))
                for u in range(G):
                    item(0, u, False, first=(u == 0))
                if p == 0:
                    dve.wait_ge(ctx_k_dma[3], 16 * 3)
                with dve.Fori(1, B - 1) as it:
                    for u in range(G):
                        item(it, u, False)
                for u in range(G):
                    item(B - 1, u, True)
                for s in range(joined(p + 1)):
                    join(p + 1, s)
                norm(B - 1, G - 1)

            for p in range(len(PHASES)):
                phase(p)
                if "att" in PHASES[p]:
                    attention(ATTS[PHASES[p]["att"]], p)

        @block.gpsimd
        def _(pool):
            def fill(tile, value):
                pool.drain()
                pool.memset(tile, value).then_inc(consts, 1)
                pool.drain()

            def clear(tile):
                fill(tile.rearrange("p a b c -> p (a b c)").bitcast(f32), 0.0)

            fill(ONES[:, :], 1.0)
            fill(HALF[:, :], -0.5)
            fill(ZERO[:, :], 0.0)
            for s in (vg_ready, max_split, rest_marked):
                pool.sem_inc(s, BIAS)
            steps = [0]

            def link(i):
                steps[0] += 1
                i.then_inc(pool_step, 1)
                pool.wait_ge(pool_step, steps[0])

            def rsqrt(var, dst, tmp, half, eps):
                link(pool.tensor_scalar(tmp, var, eps, None, ALU.add))
                return pool.tensor_tensor(dst, tmp, half, ALU.pow)

            def extra(s):
                if s == 0:
                    fill(V[:, :, :, :, :], 1.0)
                    fill(VC[:, :, :, :, :], 1.0)
                elif s == 1:
                    link(pool.memset(MTS[:, :, :], 0.0))
                    for r in range(3):
                        link(pool.affine_select(out=MTS[:, :, :], in_=MTS[:, :, :], compare_op=ALU.not_equal,
                                                fill=-1.0, base=-r, pattern=[[-3, G], [0, L]],
                                                channel_multiplier=1))
                    pool.tensor_copy(SELM[:, :, :], MTS[:, :, 0:PT])
                    pool.drain().then_inc(consts, 1)
                elif s == 2:
                    clear(KS[32:64, :, :, :])
                    clear(KS[64:PT, :, :, :])
                elif s == 3:
                    pool.wait_ge(set_dve, DVE["cstat"])
                    rsqrt(MV[0:LC, :, 1], RSTD[0:LC, 2, :], VE[0:LC, :], HALF[0:LC, :], 1e-5).then_inc(set_pool, 1)
                    pool.wait_ge(set_pool, 1)
                    clear(QS[32:64, :, :, :])
                    clear(QS[64:PT, :, :, :])

            def phase(p):
                for s in range(B):
                    pool.wait_ge(stats_ready, nth("ln", p, s))
                    if p or s >= 2:
                        pool.wait_ge(xn_ready, nth("ln", p, s) - 2)
                    if p or s:
                        pool.wait_ge(rstd_ready, nth("ln", p, s) - 1)
                    rsqrt(MV[:, :, 1], RSTD[:, s % 2, :], VE[:, :], HALF[:, :], EPS[p]).then_inc(rstd_ready, 1)
                    if p == 0:
                        extra(s)

            def attention(a, p):
                KT, KP, CM, kind = a["KT"], a["KP"], a["CM"], a["kind"]
                if PHASES[p].get("kv"):
                    pool.wait_ge(v_ready, nth("kv", p, B - 1))
                else:
                    pool.wait_ge(set_act, ACTS[f"v_{a['kc']}"])

                    pool.wait_ge(pv_done, a["u0"])
                    pool.drain()
                    pool.memset(VG[64:PT, :, :, :, :], 0.0)
                    pool.drain()

                def step(it, u, last):
                    pool.wait_ge(pv_done, it * (G * KT) + (a["u0"] + KT * (u - 3)))
                    pool.sem_inc(pool_gate, 1)
                    b = bass.ds(it, 1)
                    if kind == CROSS:
                        pool.tensor_copy(VG[0:LC, u, 0, :, 0:D + 1],
                                         VC[:, a["kc"], b, u * G:u * G + G, :].rearrange("p o h d -> p (o h) d")
                                         ).then_inc(vg_ready, 1)
                    else:
                        pool.tensor_copy(VG[:, u, :, :, 0:D + 1],
                                         V[:, b, :, u * G:u * G + G, :].rearrange("p o t h d -> p (o t) h d")
                                         ).then_inc(vg_ready, 1)
                    if a.get("topk"):
                        pool.wait_ge(t_scored, it * (2 * G * KT) + (a["t0"] + 2 * KT * (u - 3)))
                        pool.sem_inc(pool_gate, 1)
                        for c in range(CM):
                            pool.wait_ge(m_reduced, it * (G * CM) + (a["m0"] + CM * u + c + 1))
                            pool.sem_inc(pool_gate, 1)
                            pool.tensor_scalar(REST[:, u, c, :, :], TK[:, c, :, :], LOW, None, ALU.is_gt
                                               ).then_inc(rest_marked, 1)
                    pool.wait_ge(m_reduced, it * (G * CM) + (a["m0"] + CM * (u + 1)))
                    pool.sem_inc(pool_gate, 1)
                    pool.wait_ge(max_turned, it * G + (a["item0"] + u - 3))
                    pool.sem_inc(pool_gate, 1)
                    mx = V8[:, u, :, :, 0]
                    pool.tensor_copy(MP[:, u, :, :, 0], mx)
                    pool.drain()
                    pool.tensor_tensor(MRES[:, 0, :, :], mx, MP[:, u, :, :, 0], ALU.subtract)
                    pool.drain()
                    pool.tensor_copy(MP[:, u, :, :, 1], MRES[:, 0, :, :])
                    pool.drain()
                    pool.tensor_tensor(MP[:, u, :, :, 2], MRES[:, 0, :, :], MP[:, u, :, :, 1], ALU.subtract
                                       ).then_inc(max_split, 1)

                with pool.Fori(0, B) as it:
                    for u in range(G):
                        step(it, u, False)

            for s in (m_scored, max_turned, t_scored, pv_done, o_turned):
                pool.sem_inc(s, BIAS)
            for p in range(len(PHASES)):
                phase(p)
                if "att" in PHASES[p]:
                    attention(ATTS[PHASES[p]["att"]], p)


def values(steps):
    return {name: i + 1 for i, name in enumerate(steps.split())}


PES = values("vectors mod0 mod cxt k_0 v_0 gate0 gate1 mask0 mask1 mask2 mask3 gate2 gate3 k_1 v_1"
             " gate4 gate5 czt k_2 v_2 gate6 gate7 k_3 v_3")
ACTS = values("col exp cxt part1_0 v_0 gate0 gate1 part2_0 mask0 mask1 mask2 mask3 gate2 gate3 part1_1 v_1"
              " part2_1 gate4 gate5 czt part1_2 v_2 part2_2 gate6 gate7 part1_3 v_3 part2_3")
DVE = values("cond scale0 rot mask scales diag0 diag1 rest_0 diag2 diag3 part3_0 rest_1 cstat ctxn diag4 diag5"
             " part3_1 rest_2 diag6 diag7 part3_2 rest_3 part3_3")
CONSTS = values("ONES HALF ZERO V VC OWN KS32 KS64 QS32 QS64")
ACT_FROM = {p: sum(B * NT for x in STEP["mlp"] if x < p) for p in STEP["mlp"]}


def prior_write(p, s):
    if s >= 2:
        return s - 2, parts_written(p, s - 2)
    i = STEP["q"].index(p)
    return (s + 2, parts_written(STEP["q"][i - 1], s + 2)) if i else None


def kernel(**inputs):
    import concourse.bacc as _bacc
    from concourse.bass_utils import run_bass_kernel_spmd as _run

    nc = _bacc.Bacc("TRN2", target_bir_lowering=False, num_devices=1)

    def chunked(name, n):
        w = np.asarray(inputs[name])
        return w.reshape(C, n, C) if w.shape[0] == C else w.reshape(n, C, C).transpose(1, 0, 2)

    def vec(name, chunk):
        return np.asarray(inputs[name]).reshape(-1, C)[chunk]

    d = D // 2
    freq = np.float32(1.0) / np.float32(10000.0) ** (np.arange(0, D, 2, dtype=np.float32) / D)
    angle = np.outer(np.arange(L // 2, dtype=np.float32), freq)
    angle = np.concatenate([angle, angle], axis=-1)
    table = [np.tile(fn(angle).astype(np.float32).T, (H, 2)) for fn in (np.cos, np.sin)]
    odd = (np.arange(L) // WIN % 2).astype(np.float32)
    arrays = {
        "x": np.asarray(inputs["x"]), "ctx": np.asarray(inputs["ctx_1024"]),
        "mask_kv": np.asarray(inputs["mask_BxS2_bf1"]), "mask_ss": np.asarray(inputs["mask_SxS_bk0"]),
        "ada": np.concatenate([chunked(*e) for e in ADA], axis=1),
        "wts": np.concatenate([chunked(*e) for e in WTS], axis=1),
        "vecs": np.concatenate([np.asarray(inputs[n]).reshape(-1, C) for n, _ in VECS], axis=0),
        "bias_rows": np.stack([vec(*e) for e in ROWS])[None],
        "rope": np.concatenate(table, axis=1),
        "ident": np.eye(PT, dtype=np.float32),
        "side": np.stack([1 - odd, odd, NEG * odd, NEG * (1 - odd)]).astype(np.float32),
    }
    arrays = {f"in_{k}": np.ascontiguousarray(v) for k, v in arrays.items()}
    args = [nc.dram_tensor(k, v.shape, mybir.dt.from_np(v.dtype), kind="ExternalInput").ap()
            for k, v in arrays.items()]
    o = nc.dram_tensor("out_0", (B, L, C), f32, kind="ExternalOutput").ap()
    build(nc, *args, o)
    return _run(nc, [arrays], core_ids=[0]).results[0]["out_0"]
```
